# Optimizing a Trainium2 kernel written in Bass

```python
import numpy as np
import jax
import jax.numpy as jnp

def _softmax(x, axis=-1):
    return jax.nn.softmax(x, axis=axis)

def _gelu(x):
    return jax.nn.gelu(x, approximate=True)

def _silu(x):
    return jax.nn.silu(x)

def _sigmoid(x):
    return jax.nn.sigmoid(x)

def _layernorm(x, axis=-1, eps=1e-05):
    m = jnp.mean(x, axis=axis, keepdims=True)
    v = jnp.var(x, axis=axis, keepdims=True)
    return (x - m) / jnp.sqrt(v + eps)

def _scatter_add(tgt, idx, src, axis=0):
    return tgt.at[idx].add(src)

def _segment_sum(src, seg, n):
    return jax.ops.segment_sum(src, seg, n)
kernel_name = 'mk_flamingo_gated_d1_seqx_r8_5c1ed3'

def setup_inputs(seed: int=0):
    np.random.seed(seed)
    _w = jnp.asarray

    def _rec_inputs():
        import jax
        import jax.numpy as jnp
        _rk = jax.random.key(seed)
        x = -0.0002928 + 1 * jax.random.normal(jax.random.fold_in(_rk, 1), (32, 128, 128), jnp.float32)
        _lenS = 128 - jax.random.randint(jax.random.fold_in(_rk, 7), (32,), 0, max(1, 128 // 4) + 1, jnp.int32)
        _lenS2 = 128 - jax.random.randint(jax.random.fold_in(_rk, 8), (32,), 0, max(1, 128 // 4) + 1, jnp.int32)
        _ctx_1024P = jax.random.normal(jax.random.fold_in(_rk, 11), (32, 16, 128), jnp.float32)
        _ctx_1024c = jax.random.dirichlet(jax.random.fold_in(_rk, 511), 0.3 * jnp.ones((16,), jnp.float32), (32, 128))
        _ctx_1024t = jnp.einsum('bsk,bkd->bsd', _ctx_1024c, _ctx_1024P)
        _ctx_1024t = _ctx_1024t * jax.lax.rsqrt(jnp.mean(jnp.square(_ctx_1024t)) + 1e-12) * 0.953939
        ctx_1024 = -1.39393e-06 + 0.999914 * (_ctx_1024t + 0.3 * jax.random.normal(jax.random.fold_in(_rk, 611), (32, 128, 128), jnp.float32))
        _validS = jnp.arange(128)[None, :] < _lenS[:, None]
        _validS2 = jnp.arange(128)[None, :] < _lenS2[:, None]
        _causal = jnp.tril(jnp.ones((128, 128), dtype=bool))
        mask_BxSxS2_bk1 = jnp.broadcast_to(_validS2[:, None, :], (32, 128, 128))
        _g = jax.random.normal(jax.random.fold_in(_rk, 9001), (2, 1), jnp.float32)
        _g = jnp.sign(_g) * jnp.maximum(jnp.abs(_g), 1.0) + (_g == 0) * 1.0
        g_xattn = _g[0]
        g_ffn = _g[1]
        return (x, ctx_1024, mask_BxSxS2_bk1, g_xattn, g_ffn)
    x, ctx_1024, mask_BxSxS2_bk1, g_xattn, g_ffn = _rec_inputs()

    def _L0_xattn_setup():
        import jax, jax.numpy as jnp
        import numpy as np
        B, S, D, H = (2, 256, 128, 16)
        HD = D // H

        def _split_heads(x):
            b, s, _ = x.shape
            return x.reshape(b, s, H, HD).transpose(0, 2, 1, 3)
        key = jax.random.key(seed)
        ks = jax.random.split(key, 12)
        scale = 1.0 / np.sqrt(D)
        inp = {'query': jax.random.normal(ks[0], (B, S, D), jnp.float32), 'key': jax.random.normal(ks[1], (B, S, D), jnp.float32), 'value': jax.random.normal(ks[2], (B, S, D), jnp.float32), 'mask': jnp.broadcast_to(jnp.triu(jnp.ones((S, S), jnp.bool_), k=1), (B, S, S)), 'Wq': jax.random.normal(ks[3], (D, D), jnp.float32) * scale, 'bq': jnp.zeros((D,), jnp.float32), 'Wk': jax.random.normal(ks[4], (D, D), jnp.float32) * scale, 'bk': jnp.zeros((D,), jnp.float32), 'Wv': jax.random.normal(ks[5], (D, D), jnp.float32) * scale, 'bv': jnp.zeros((D,), jnp.float32), 'Wo': jax.random.normal(ks[6], (D, D), jnp.float32) * scale, 'bo': jnp.zeros((D,), jnp.float32)}
        return inp
    _L0_xattn_all = _L0_xattn_setup()
    _L0_xattn_in = {k: v for k, v in _L0_xattn_all.items() if k in ('Wq', 'bq', 'Wk', 'bk', 'Wv', 'bv', 'Wo', 'bo')}
    del _L0_xattn_all

    def _L0_ffn_setup():
        import jax, jax.numpy as jnp
        import numpy as np
        MAX_THRESHOLD = 0.125
        key = jax.random.key(seed)
        ks = jax.random.split(key, 5)
        B, S, D, FF, E = (2, 256, 128, 512, 8)
        sd = 1.0 / np.sqrt(D)
        sf = 1.0 / np.sqrt(FF)
        return {'inputs': jax.random.normal(ks[0], (B, S, D), dtype=jnp.float32), 'Wg': jax.random.normal(ks[1], (D, E), dtype=jnp.float32) * sd, 'bg': jnp.zeros((E,), dtype=jnp.float32), 'Wt': jax.random.normal(ks[2], (D, 1), dtype=jnp.float32) * sd, 'bt': jnp.zeros((1,), dtype=jnp.float32), 'W1': jax.random.normal(ks[3], (E, D, FF), dtype=jnp.float32) * sd, 'b1': jnp.zeros((E, FF), dtype=jnp.float32), 'W2': jax.random.normal(ks[4], (E, FF, D), dtype=jnp.float32) * sf, 'b2': jnp.zeros((E, D), dtype=jnp.float32)}
    _L0_ffn_all = _L0_ffn_setup()
    _L0_ffn_in = {k: v for k, v in _L0_ffn_all.items() if k in ('Wg', 'bg', 'Wt', 'bt', 'W1', 'b1', 'W2', 'b2')}
    del _L0_ffn_all
    return {'x': x, 'ctx_1024': ctx_1024, 'mask_BxSxS2_bk1': mask_BxSxS2_bk1, 'g_xattn': g_xattn, 'g_ffn': g_ffn, 'L0_xattn_Wq': _L0_xattn_in['Wq'], 'L0_xattn_bq': _L0_xattn_in['bq'], 'L0_xattn_Wk': _L0_xattn_in['Wk'], 'L0_xattn_bk': _L0_xattn_in['bk'], 'L0_xattn_Wv': _L0_xattn_in['Wv'], 'L0_xattn_bv': _L0_xattn_in['bv'], 'L0_xattn_Wo': _L0_xattn_in['Wo'], 'L0_xattn_bo': _L0_xattn_in['bo'], 'L0_ffn_Wg': _L0_ffn_in['Wg'], 'L0_ffn_bg': _L0_ffn_in['bg'], 'L0_ffn_Wt': _L0_ffn_in['Wt'], 'L0_ffn_bt': _L0_ffn_in['bt'], 'L0_ffn_W1': _L0_ffn_in['W1'], 'L0_ffn_b1': _L0_ffn_in['b1'], 'L0_ffn_W2': _L0_ffn_in['W2'], 'L0_ffn_b2': _L0_ffn_in['b2']}

def reference(x, ctx_1024, mask_BxSxS2_bk1, g_xattn, g_ffn, L0_xattn_Wq, L0_xattn_bq, L0_xattn_Wk, L0_xattn_bk, L0_xattn_Wv, L0_xattn_bv, L0_xattn_Wo, L0_xattn_bo, L0_ffn_Wg, L0_ffn_bg, L0_ffn_Wt, L0_ffn_bt, L0_ffn_W1, L0_ffn_b1, L0_ffn_W2, L0_ffn_b2):
    import jax
    import jax.numpy as jnp

    def _L0_xattn_ref(query, key, value, mask, Wq, bq, Wk, bk, Wv, bv, Wo, bo):
        import jax, jax.numpy as jnp
        import numpy as np
        B, S, D, H = (2, 256, 128, 16)
        HD = D // H

        def _split_heads(x):
            b, s, _ = x.shape
            return x.reshape(b, s, H, HD).transpose(0, 2, 1, 3)
        q = _split_heads(query @ Wq.T + bq)
        k = _split_heads(key @ Wk.T + bk)
        v = _split_heads(value @ Wv.T + bv)
        scores = jnp.einsum('bhqd,bhkd->bhqk', q, k) / jnp.sqrt(jnp.float32(HD))
        scores = jnp.where(mask[:, None, :, :], jnp.finfo(scores.dtype).min, scores)
        attn = jax.nn.softmax(scores, axis=-1)
        ctx = jnp.einsum('bhqk,bhkd->bhqd', attn, v)
        merged = ctx.transpose(0, 2, 1, 3).reshape(query.shape[0], -1, D)
        out = merged @ Wo.T + bo
        return out

    def _L0_ffn_ref(inputs, Wg, bg, Wt, bt, W1, b1, W2, b2):
        import jax, jax.numpy as jnp
        import numpy as np
        MAX_THRESHOLD = 0.125
        x = inputs.reshape(-1, inputs.shape[-1])
        gate = jax.nn.softmax(x @ Wg + bg, axis=-1)
        thr = jax.nn.sigmoid(x @ Wt + bt) * MAX_THRESHOLD
        adapted = gate - thr
        mask = (adapted >= 0).astype(x.dtype)
        w = adapted * mask
        s = jnp.sum(w, axis=-1, keepdims=True)
        s = jnp.where(s == 0, jnp.ones_like(s), s)
        w = w / s
        h = jax.nn.gelu(jnp.einsum('td,edf->etf', x, W1) + b1[:, None, :])
        eo = jnp.einsum('etf,efd->etd', h, W2) + b2[:, None, :]
        out = jnp.einsum('te,etd->td', w, eo)
        return out.reshape(inputs.shape)
    x = x + jnp.tanh(g_xattn[0]) * _L0_xattn_ref(_layernorm(x, axis=-1), ctx_1024, ctx_1024, mask_BxSxS2_bk1, L0_xattn_Wq, L0_xattn_bq, L0_xattn_Wk, L0_xattn_bk, L0_xattn_Wv, L0_xattn_bv, L0_xattn_Wo, L0_xattn_bo)
    x = x + jnp.tanh(g_ffn[0]) * _L0_ffn_ref(_layernorm(x, axis=-1), L0_ffn_Wg, L0_ffn_bg, L0_ffn_Wt, L0_ffn_bt, L0_ffn_W1, L0_ffn_b1, L0_ffn_W2, L0_ffn_b2)
    return x

_drawn_inputs = setup_inputs


def setup_inputs(seed=0):
    import zlib

    import numpy as np

    out = dict(_drawn_inputs(seed))
    spreads = {'L0_xattn_bq': (0.0, 0.363),
     'L0_xattn_bk': (0.0, 0.8),
     'L0_xattn_bv': (0.0, 0.1),
     'L0_xattn_bo': (0.0, 0.1),
     'L0_ffn_bg': (0.0, 0.365),
     'L0_ffn_b1': (0.0, 0.1),
     'L0_ffn_b2': (0.0, 0.1)}
    factors = {}
    for name, (base, spread) in spreads.items():
        noise = np.random.default_rng([zlib.crc32(name.encode()), seed]).standard_normal(out[name].shape)
        drawn = base * np.exp(spread * noise) if base else spread * noise
        out[name] = jnp.asarray(drawn.astype(out[name].dtype))
    for name, factor in factors.items():
        out[name] = (out[name] * factor).astype(out[name].dtype)
    return out
```

```python
from contextlib import ExitStack

import concourse.bass as bass
from concourse import mybir

F32 = mybir.dt.float32
F32R = mybir.dt.float32r
BF16 = mybir.dt.bfloat16
U8 = mybir.dt.uint8
I32 = mybir.dt.int32
ALU = mybir.AluOpType
ACT = mybir.ActivationFunctionType
AX = mybir.AxisListType

P = 128
B, S, D = 32, 128, 128
H, HD = 16, 8
E, FF = 8, 512
TOK = B * S
GB = 2
GT = GB * S
NG = B // GB
SLABS, ROWS = 4, 4
COMBOS = 4
FC = FF // P
CH = E * FC
BT = 512
NB = TOK // BT
TPB = BT // P
LAG = 4
HBUF = 8
NGATE = E + 1
EPS = 1e-5
SCALE = float(HD) ** -0.5
MASKED = -(2.0 ** 126)
MAX_THRESHOLD = 0.125
NW = 2 * E

BANKS = [["max", "p23", "x2T", "gate", "merged"],
         ["ctxT", "p01", "p67", "heads"],
         ["xT", "p45", "v", "wo"]]
OF_CUR = {"max", "heads", "merged", "wo"}
OF_PRV = {"x2T", "gate"}


def bank_of(what):
    return [what in order for order in BANKS].index(True)


def fills(what, it):
    prv, cur, nxt = it
    order = BANKS[bank_of(what)]
    present = [w for w in order if (prv if w in OF_PRV else cur if w in OF_CUR else nxt) is not None]
    n_prv = sum(w in OF_PRV for w in order)
    n_cur = sum(w in OF_CUR for w in order)
    n_nxt = len(order) - n_prv - n_cur
    at = present.index(what) + 1
    if cur is None and prv is None:
        return at
    if cur is None:
        return n_nxt * NG + n_cur * NG + n_prv * (NG - 1) + at
    if nxt is None:
        return n_nxt * NG + n_cur * (NG - 1) + n_prv * (NG - 2) + at
    if prv is None:
        return n_nxt + at
    return cur * len(order) + (n_nxt - n_prv + at)


def gated_block(nc, a):
    ctx = ExitStack()
    phase_a = ExitStack()
    phase_b = ExitStack()
    with ctx:
        def sb(name, shape, dt, stack=ctx):
            return stack.enter_context(nc.sbuf_tensor(name, shape, dt))

        def sem(name):
            return ctx.enter_context(nc.semaphore(name))

        x_all = sb("x_all", [P, B, D], F32)
        x2_high = sb("x2_high", [P, TOK], F32R)
        x2_low = sb("x2_low", [P, TOK], F32R)
        w_high = sb("w_high", [P, NW, 512], F32R)
        w_low = sb("w_low", [P, NW, 512], F32R)
        b1_sb = sb("b1_sb", [P, CH], F32)
        b2_sb = sb("b2_sb", [P, E], F32)
        ident = sb("ident_sb", [P, P], F32)
        ident_b = sb("ident_b", [P, P], BF16)
        gates = sb("gates", [P, 2], F32)
        tanh_g = sb("tanh_g", [P, 2], F32)

        def sa(name, shape, dt):
            return sb(name, shape, dt, phase_a)
        k_masked = sa("k_masked", [P, SLABS, ROWS, GT], F32R)
        q_masked = sa("q_masked", [P, SLABS, ROWS, GT], F32R)
        k_stack = sa("k_stack", [P, SLABS, GT], F32R)
        q_stack = sa("q_stack", [P, SLABS, GT], F32R)
        k_cur = sa("k_cur", [P, SLABS, GT], F32R)
        probs = sa("probs", [P, 2, 8 * S], F32)
        v_pad = sa("v_pad", [P, GB, H, 32], F32)
        ctx_sb = sa("ctx_sb", [P, GB, D], F32)
        xn = sa("xn", [P, GB, D], F32)
        xT_high = sa("xT_high", [P, GT], F32R)
        xT_low = sa("xT_low", [P, GT], F32R)
        ctxT_high = sa("ctxT_high", [P, GT], F32R)
        ctxT_low = sa("ctxT_low", [P, GT], F32R)
        part = sa("part", [P, 4, GT], F32R)
        mask_words = sa("mask_words", [P, GB, S // 4], I32)
        mask_nxt = sa("mask_nxt", [P, GB, S], BF16)
        mask_cur = sa("mask_cur", [P, GB, S], BF16)
        masked_ident = sa("masked_ident", [P, P], BF16)
        wqk_raw = probs[:, 0, 0:2 * SLABS * P]
        wv_raw = probs[:, 1, 0:P]
        wqk_high = sa("wqk_high", [P, 2 * SLABS * P], F32R)
        wqk_low = sa("wqk_low", [P, 2 * SLABS * P], F32R)
        wv_high = sa("wv_high", [P, P], F32R)
        wv_low = sa("wv_low", [P, P], F32R)
        wo_sb = sa("wo_sb", [P, P], F32)
        bqk = sa("bqk", [P, 2 * SLABS], F32)
        bqk_low = sa("bqk_low", [P, 2 * SLABS], F32)
        low_rows = sa("low_rows_sb", [P, 2 * SLABS], F32)
        bv_row = sa("bv_row", [P, P], F32)
        bo_row = sa("bo_row", [P, P], F32)
        bg_row = sa("bg_row", [P, NGATE], F32)
        wg_sb = sa("wg_sb", [P, NGATE], F32)
        stats = sa("stats", [P, B, 6], F32)
        mean_var = sa("mean_var", [P, B, 2], F32)
        rstd = sa("rstd", [P, B], F32)
        shift = sa("shift", [P, B], F32)
        power = sa("power", [P, B], F32)
        neg_max = sa("neg_max", [P, GB, H], F32)
        max_parts = sa("max_parts", [P, GB, 2 * H], F32R)
        maxT = sa("maxT", [2 * H, GT], F32R)
        headsT = sa("headsT", [P, GB, 2 * P], F32)
        sums_r = sa("sums_r", [P, GB * H], F32)
        merged = sa("merged", [P, GB * H, HD], F32)
        mergedT = sa("mergedT", [P, GT], F32)
        x_biased = sa("x_biased", [P, GB, D], F32)
        stats2 = sa("stats2", [P, GB, 6], F32)
        mean_var2 = sa("mean_var2", [P, GB, 2], F32)
        rstd2 = sa("rstd2", [P, GB], F32)
        x2n = sa("x2n", [P, GB, D], F32)
        x2T = sa("x2T_sb", [P, GT], F32)
        w_raw = sa("w_raw", [P, 512], F32)
        logits = sa("logits", [P, B, NGATE], F32)
        g_max = sa("g_max", [P, B], F32)
        g_exp = sa("g_exp", [P, B, E], F32)
        g_sum = sa("g_sum", [P, B], F32)
        g_thr = sa("g_thr", [P, B], F32)
        w_parts = sa("w_parts", [P, B, 3 * E], BF16)
        phase_a.close()

        def sbb(name, shape, dt):
            return sb(name, shape, dt, phase_b)
        expert_wT = sbb("expert_wT", [P, TOK], BF16)
        sel_words = sbb("sel_words", [P, E * P // 4], I32)
        sel = sbb("sel_b", [P, E, P], BF16)
        h_sb = sbb("h_sb", [P, HBUF, BT], F32)
        h_high = sbb("h_high", [P, HBUF, BT], F32R)
        h_low = sbb("h_low", [P, HBUF, BT], F32R)
        w_row = sbb("w_row", [P, 2, BT], F32)
        weighted = sbb("weighted", [P, 2, BT], F32)
        yT = sbb("yT", [P, BT], F32)
        y_out = sbb("y_out", [P, TPB, D], F32)
        phase_b.close()

        psum_a = ExitStack()
        scores = psum_a.enter_context(nc.psum_tensor("scores", [P, 4, 512], F32))
        misc = psum_a.enter_context(nc.psum_tensor("misc", [P, 3, 512], F32))
        heads = psum_a.enter_context(nc.psum_tensor("heads", [P, GB, 256], F32))
        psum_a.close()
        psum_b = ExitStack()
        ps_h = psum_b.enter_context(nc.psum_tensor("ps_h", [P, 4, BT], F32))
        ps_w = psum_b.enter_context(nc.psum_tensor("ps_w", [P, BT], F32))
        ps_t = psum_b.enter_context(nc.psum_tensor("ps_t", [P, TPB, D], F32))
        ps_y = psum_b.enter_context(nc.psum_tensor("ps_y", [P, 2, BT], F32))
        psum_b.close()
        psum_g = ExitStack()
        ps_wT = psum_g.enter_context(nc.psum_tensor("ps_wT", [P, 4, 1024], BF16))
        psum_g.close()

        x_in = sem("x_in")
        x_rest_in = sem("x_rest_in")
        waited = sem("waited")
        wts_in = sem("wts_in")
        ctx_in = sem("ctx_in")
        mask_in = sem("mask_in")
        w_in = sem("w_in")
        sel_in = sem("sel_in")
        const_pool = sem("const_pool")
        const_act = sem("const_act")
        bias_low_done = sem("bias_low_done")
        qk_w_done = sem("qk_w_done")
        ln1_stats = sem("ln1_stats")
        ln1_aggr = sem("ln1_aggr")
        ln1_pool = sem("ln1_pool")
        ln1_done = sem("ln1_done")
        pad_done = sem("pad_done")
        xn_scaled = sem("xn_scaled")
        xn_done = sem("xn_done")
        high_done = sem("high_done")
        part_done = sem("part_done")
        misc_full = [sem("misc0_full"), sem("misc1_full"), sem("misc2_full")]
        misc_read = [sem("misc0_read"), sem("misc1_read"), sem("misc2_read")]
        scores_full = [sem("scores0_full"), sem("scores1_full")]
        scores_read = [sem("scores0_read"), sem("scores1_read")]
        probs_done = [sem("probs0_done"), sem("probs1_done")]
        pv_done = [sem("pv0_done"), sem("pv1_done")]
        headsT_done = sem("headsT_done")
        km_in = sem("km_in")
        kcur_in = sem("kcur_in")
        qm_in = sem("qm_in")
        max_in = sem("max_in")
        maxhigh_done = sem("maxhigh_done")
        max_done = sem("max_done")
        recip_done = sem("recip_done")
        merged_done = sem("merged_done")
        biased_done = sem("biased_done")
        x1_done = sem("x1_done")
        stats2_done = sem("stats2_done")
        aggr2_done = sem("aggr2_done")
        var2_done = sem("var2_done")
        rstd2_done = sem("rstd2_done")
        x2n_done = sem("x2n_done")
        x2T_done = sem("x2T_done")
        x2high_done = sem("x2high_done")
        x2low_done = sem("x2low_done")
        masknxt_done = sem("masknxt_done")
        maskcur_done = sem("maskcur_done")
        wsplit_high = sem("wsplit_high")
        wsplit_done = sem("wsplit_done")
        g_dve = sem("g_dve")
        g_act = sem("g_act")
        g_full = sem("g_full")
        wT_zeroed = sem("wT_zeroed")
        g_copied = sem("g_copied")
        sel_done = sem("sel_done")
        h_full = sem("h_full")
        h_done = sem("h_done")
        high2_done = sem("high2_done")
        low2_done = sem("low2_done")
        w2_done = sem("w2_done")
        wrow_full = sem("wrow_full")
        wrow_done = sem("wrow_done")
        weighted_done = sem("weighted_done")
        added = sem("added")
        t_full = sem("t_full")
        t_read = sem("t_read")
        y_stored = sem("y_stored")

        block = ctx.enter_context(nc.Block())

        N_WTS = 14 * 16

        def settle(eng):
            eng.sem_inc(waited, 1)

        def misc_wait_full(eng, what, it):
            k = bank_of(what)
            eng.wait_ge(misc_full[k], fills(what, it))

        def misc_wait_read(eng, what, it):
            k = bank_of(what)
            eng.wait_ge(misc_read[k], fills(what, it))

        def misc_wait_free(eng, what, it):
            k = bank_of(what)
            n = fills(what, it)
            if not (isinstance(n, int) and n == 1):
                eng.wait_ge(misc_read[k], n - 1)

        def wait_count(eng, s, n):
            if not (isinstance(n, int) and n <= 0):
                eng.wait_ge(s, n)

        def fill_T(cur, b):
            return cur * (2 * GB) + (GB + b + 1)

        def fill_N(cur, b):
            return b + 1 if cur is None else cur * (2 * GB) + (2 * GB + b + 1)

        def natural_over(group):
            return group * (2 * GB) + GB

        def loop(eng, body):
            body(None, None, 0)
            body(None, 0, 1)
            body(0, 1, 2)
            with eng.Fori(2, NG - 1) as cur:
                body(cur - 1, cur, cur + 1)
            body(NG - 2, NG - 1, None)
            body(NG - 1, None, None)

        def wait_spare_loads(eng):
            eng.wait_ge(ctx_in, 16 * (NG + 1))
            eng.wait_ge(mask_in, 16 * (NG + 1))
            eng.wait_ge(w_in, 16 * (NG + 1))

        def loop_b(eng, body):
            body(0)
            body(1)
            with eng.Fori(2, NB) as g:
                body(g)

        @block.sync
        def _(sp):
            ctx_v = a["ctx"].rearrange("(g b p) d -> g p b d", p=P, b=GB)
            mask_v = a["mask"].rearrange("(g b) q k -> g q b k", b=GB)
            sp.dma_start(x_all[:, 0:GB, :], a["x"][0:GB * S, :].rearrange("(b p) d -> p b d", p=P)).then_inc(x_in, 16)
            sp.dma_start(ident[:], a["ident"]).then_inc(wts_in, 16)
            sp.dma_start(ctx_sb[:], ctx_v[0]).then_inc(ctx_in, 16)
            sp.dma_start(mask_words[:], mask_v[0]).then_inc(mask_in, 16)
            sp.dma_start(wqk_raw[:, SLABS * P:], a["wqk"][:, SLABS * P:]).then_inc(wts_in, 16)
            sp.dma_start(wqk_raw[:, 0:SLABS * P], a["wqk"][:, 0:SLABS * P]).then_inc(wts_in, 16)
            sp.dma_start(bqk[:], a["bqk"]).then_inc(wts_in, 16)
            sp.dma_start(low_rows[:], a["low_rows"]).then_inc(wts_in, 16)
            sp.dma_start(wv_raw, a["wvT"]).then_inc(wts_in, 16)
            sp.dma_start(bv_row[:], a["bv"].partition_broadcast(P)).then_inc(wts_in, 16)
            sp.dma_start(gates[:], a["g"].partition_broadcast(P)).then_inc(wts_in, 16)
            sp.dma_start(bo_row[:], a["bo"].partition_broadcast(P)).then_inc(wts_in, 16)
            sp.dma_start(wo_sb[:], a["woT"]).then_inc(wts_in, 16)
            sp.dma_start(wg_sb[:], a["wg"]).then_inc(wts_in, 16)
            sp.dma_start(bg_row[:], a["bg"].partition_broadcast(P)).then_inc(wts_in, 16)
            sp.dma_start(b1_sb[:], a["b1"]).then_inc(wts_in, 16)
            sp.dma_start(b2_sb[:], a["b2"]).then_inc(wts_in, 16)
            sp.dma_start(w_raw[:], a["w_ffn"][0]).then_inc(w_in, 16)
            sp.dma_start(x_all[:, GB:, :], a["x"][GB * S:, :].rearrange("(b p) d -> p b d", p=P)).then_inc(x_rest_in, 16)

            def body(prv, cur, nxt):
                it = (prv, cur, nxt)
                if cur is not None:
                    misc_wait_read(sp, "max", it)
                    settle(sp)
                    for j in range(2):
                        sp.dma_start(q_masked[24 + j:25 + j, :, :, :].rearrange("p s r q -> p (s r) q").bitcast(F32),
                                     maxT[H * j:H * j + H, :].bitcast(F32)).then_inc(max_in, 16)
                if nxt is not None:
                    misc_wait_read(sp, "p01", it)
                    settle(sp)
                    misc_wait_read(sp, "p23", it)
                    settle(sp)
                    if cur is not None:
                        sp.wait_ge(scores_full[1], natural_over(cur))
                        settle(sp)
                    else:
                        sp.wait_ge(pad_done, 2)
                    for r in range(ROWS):
                        rows = slice(32 * r, 32 * r + 32)
                        sp.dma_start(k_masked[rows, :, r, :].bitcast(F32), k_stack[rows, :, :].bitcast(F32)).then_inc(km_in, 16)
                    misc_wait_read(sp, "p45", it)
                    settle(sp)
                    misc_wait_read(sp, "p67", it)
                    settle(sp)
                    if cur is not None:
                        sp.wait_ge(scores_full[1], fill_T(cur, GB - 1))
                        settle(sp)
                    sp.dma_start(k_cur[:].bitcast(F32), k_stack[:].bitcast(F32)).then_inc(kcur_in, 16)
                    for r in range(ROWS):
                        rows = slice(32 * r, 32 * r + 24)
                        sp.dma_start(q_masked[rows, :, r, :].bitcast(F32), q_stack[rows, :, :].bitcast(F32)).then_inc(qm_in, 16)
                    dyn = prv is not None and not isinstance(prv, int)
                    ahead = cur + 2 if dyn else nxt + 1
                    at = bass.ds(ahead, 1) if dyn else ahead
                    misc_wait_full(sp, "ctxT", it)
                    settle(sp)
                    sp.dma_start(ctx_sb[:], ctx_v[at]).then_inc(ctx_in, 16)
                    sp.wait_ge(maskcur_done, nxt + 1)
                    settle(sp)
                    sp.dma_start(mask_words[:], mask_v[at]).then_inc(mask_in, 16)
                    sp.wait_ge(wsplit_done, nxt + 1)
                    settle(sp)
                    sp.dma_start(w_raw[:], a["w_ffn"][at]).then_inc(w_in, 16)
            loop(sp, body)
            out_v = a["out"].rearrange("(g t p) d -> g p t d", p=P, t=TPB)
            with sp.Fori(0, NB) as g:
                sp.wait_ge(t_read, g + 1)
                settle(sp)
                sp.dma_start(out_v[g], y_out[:]).then_inc(y_stored, 16)
            sp.wait_ge(y_stored, 16 * NB)

        @block.gpsimd
        def _(pool):
            nc.gpsimd.memset(power[:], -0.5).then_inc(const_pool, 1)
            nc.gpsimd.memset(v_pad[:], 0.0).then_inc(const_pool, 1)
            pool.wait_ge(const_pool, 2)
            vv = v_pad[:].rearrange("p b (hh o) c -> p (b hh) o c", o=2)
            nc.gpsimd.memset(vv[:, :, 0, 8:16], 1.0).then_inc(const_pool, 1)
            nc.gpsimd.memset(vv[:, :, 1, 24:32], 1.0).then_inc(const_pool, 1)
            for n, (lo, hi) in enumerate(((0, GB), (GB, B))):
                pool.wait_ge(ln1_aggr, hi)
                nc.gpsimd.tensor_scalar(rstd[:, lo:hi], mean_var[:, lo:hi, 1], EPS, 1.0, ALU.add, ALU.mult).then_inc(ln1_pool, 1)
                pool.wait_ge(ln1_pool, 4 * n + 1)
                nc.gpsimd.tensor_tensor(rstd[:, lo:hi], rstd[:, lo:hi], power[:, lo:hi], ALU.pow).then_inc(ln1_pool, 1)
                pool.wait_ge(ln1_pool, 4 * n + 2)
                nc.gpsimd.tensor_tensor(shift[:, lo:hi], mean_var[:, lo:hi, 0], rstd[:, lo:hi], ALU.mult).then_inc(ln1_pool, 1)
                pool.wait_ge(ln1_pool, 4 * n + 3)
                nc.gpsimd.tensor_scalar(shift[:, lo:hi], shift[:, lo:hi], -1.0, 0.0, ALU.mult, ALU.add).then_inc(ln1_pool, 1)
                pool.wait_ge(ln1_pool, 4 * n + 4)
                if n == 0:
                    for b in range(GB):
                        nc.gpsimd.tensor_scalar(xn[:, b, :], x_all[:, b, :], rstd[:, b:b + 1], shift[:, b:b + 1],
                                                ALU.mult, ALU.add).then_inc(xn_done, 1)
                    pool.wait_ge(wts_in, N_WTS)
                    pool.wait_ge(qk_w_done, 1)
                    nc.gpsimd.tensor_scalar(bo_row[:], bo_row[:], tanh_g[:, 0:1], 0.0, ALU.mult, ALU.add).then_inc(const_pool, 1)

            def body(prv, cur, nxt):
                if nxt is not None:
                    if cur is not None:
                        last = {None: (None, None, 0), 0: (None, 0, 1)}.get(prv if prv is None or isinstance(prv, int) else "x")
                        k = bank_of("xT")
                        pool.wait_ge(misc_full[k], fills("xT", last) if last else (cur - 1) * len(BANKS[k]) + fills("xT", (0, 0, 0)))
                        settle(pool)
                        ts = bass.ds(cur * GB + GB, GB)
                        nc.gpsimd.tensor_tensor(xn[:], x_all[:, ts, :], rstd[:, ts].unsqueeze(2).to_broadcast([P, GB, D]),
                                                ALU.mult).then_inc(xn_scaled, 1)
                        pool.wait_ge(xn_scaled, cur + 1)
                        settle(pool)
                        nc.gpsimd.tensor_tensor(xn[:], xn[:], shift[:, ts].unsqueeze(2).to_broadcast([P, GB, D]),
                                                ALU.add).then_inc(xn_done, GB)
                if cur is not None:
                    if not (isinstance(cur, int) and cur == 0):
                        pool.wait_ge(misc_read[2], fills("xT" if nxt is not None else "wo", (prv, cur, nxt)) - 1)
                        settle(pool)
                    nc.gpsimd.tensor_tensor(x_biased[:], x_all[:, bass.ds(cur * GB, GB), :],
                                            bo_row[:].unsqueeze(1).to_broadcast([P, GB, D]), ALU.add).then_inc(biased_done, 1)
                if prv is not None:
                    pool.wait_ge(var2_done, prv + 1)
                    settle(pool)
                    nc.gpsimd.tensor_tensor(rstd2[:], rstd2[:], power[:, 0:GB], ALU.pow).then_inc(rstd2_done, 1)
                if nxt is not None:
                    if cur is not None:
                        pool.wait_ge(scores_full[1], natural_over(cur))
                        settle(pool)
                    pool.wait_ge(mask_in, 16 * nxt + 16)
                    settle(pool)
                    nc.gpsimd.tensor_copy(mask_nxt[:], mask_words[:].bitcast(U8)).then_inc(masknxt_done, 1)
                    pool.wait_ge(w_in, 16 * nxt + 16)
                    settle(pool)
                    nc.gpsimd.tensor_copy(w_high[:, bass.ds(nxt, 1), :], w_raw[:]).then_inc(wsplit_high, 1)
                    pool.wait_ge(wsplit_high, nxt + 1)
                    settle(pool)
                    nc.gpsimd.tensor_tensor(w_low[:, bass.ds(nxt, 1), :], w_raw[:],
                                            w_high[:, bass.ds(nxt, 1), :].bitcast(F32), ALU.subtract).then_inc(wsplit_done, 1)
                    if cur is not None:
                        pool.wait_ge(scores_full[1], fill_T(cur, GB - 1))
                        settle(pool)
                    nc.gpsimd.tensor_copy(mask_cur[:], mask_words[:].bitcast(U8)).then_inc(maskcur_done, 1)
                if prv is not None:
                    pool.wait_ge(x2high_done, prv + 1)
                    settle(pool)
                    nc.gpsimd.tensor_tensor(x2_low[:, bass.ds(prv * GT, GT)], x2T[:],
                                            x2_high[:, bass.ds(prv * GT, GT)].bitcast(F32), ALU.subtract).then_inc(x2low_done, 1)
            pool.wait_ge(const_pool, 5)
            loop(pool, body)

            wait_spare_loads(pool)
            pool.wait_ge(x2high_done, NG)
            nc.gpsimd.memset(expert_wT[:], 0.0).then_inc(wT_zeroed, 1)
            nc.gpsimd.dma_start(sel_words[:], a["sel"]).then_inc(sel_in, 16)
            pool.wait_ge(sel_in, 16)
            nc.gpsimd.tensor_copy(sel[:].rearrange("p e m -> p (e m)"), sel_words[:].bitcast(U8)).then_inc(sel_done, 1)

            def body_b(g):
                for e in range(1, E):
                    pool.wait_ge(weighted_done, g * E + (e + 1))
                    if e > 1:
                        pool.wait_ge(added, g * (E - 1) + (e - 1))
                    nc.gpsimd.tensor_tensor(yT[:], yT[:], weighted[:, e % 2, :], ALU.add).then_inc(added, 1)
            loop_b(pool, body_b)

        @block.scalar
        def _(act):
            act.wait_ge(wts_in, N_WTS)
            nc.scalar.activation(tanh_g[:], gates[:], ACT.Tanh).then_inc(qk_w_done, 1)
            nc.scalar.activation(wqk_high[:, SLABS * P:], wqk_raw[:, SLABS * P:], ACT.Copy).then_inc(qk_w_done, 1)
            nc.scalar.activation(wqk_high[:, 0:SLABS * P], wqk_raw[:, 0:SLABS * P], ACT.Copy).then_inc(qk_w_done, 1)
            nc.scalar.activation(wv_high[:], wv_raw, ACT.Copy).then_inc(qk_w_done, 1)
            nc.scalar.activation(ident_b[:], ident[:], ACT.Copy).then_inc(const_act, 1)
            nc.scalar.activation(masked_ident[:], ident[:], ACT.Copy, scale=MASKED).then_inc(const_act, 1)

            def exp_half(cur, b, u):
                act.wait_ge(scores_full[u], fill_T(cur, b))
                wait_count(act, pv_done[u], cur * GB + b)
                nc.scalar.activation(probs[:, u, :], scores[:, 2 * u:2 * u + 2, :].rearrange("p a c -> p (a c)"),
                                     ACT.Exp, scale=SCALE).then_inc(scores_read[u], 1)

            def body(prv, cur, nxt):
                it = (prv, cur, nxt)

                def high(dst, what):
                    misc_wait_full(act, what, it)
                    nc.scalar.activation(dst[:], misc[:, bank_of(what), 0:GT], ACT.Copy).then_inc(high_done, 1)

                def parts(i):
                    what = f"p{i}{i + 1}"
                    misc_wait_full(act, what, it)
                    if i >= SLABS:
                        misc_wait_read(act, f"p{i - 4}{i - 3}", it)
                    for k in range(2):
                        nc.scalar.activation(part[:, (i + k) % 4, :], misc[:, bank_of(what), k * GT:(k + 1) * GT], ACT.Identity,
                                             scale=low_rows[:, i + k:i + k + 1],
                                             bias=bqk_low[:, i + k:i + k + 1]).then_inc(part_done, 1)

                if nxt is not None:
                    high(ctxT_high, "ctxT")
                if cur is not None:
                    misc_wait_full(act, "max", it)
                    wait_count(act, max_in, cur * 32)
                    nc.scalar.activation(maxT[:], misc[0:2 * H, bank_of("max"), 0:GT], ACT.Copy).then_inc(misc_read[0], 1)
                if nxt is not None:
                    high(xT_high, "xT")
                    if cur is None:
                        act.wait_ge(bias_low_done, 1)
                    parts(0)
                    parts(2)
                if cur is not None:
                    exp_half(cur, 0, 0)
                if nxt is not None:
                    parts(4)
                if cur is not None:
                    exp_half(cur, 0, 1)
                if nxt is not None:
                    parts(6)
                if cur is not None:
                    exp_half(cur, 1, 0)
                    exp_half(cur, 1, 1)
                if prv is not None:
                    misc_wait_full(act, "x2T", it)
                    wait_count(act, x2low_done, prv)
                    nc.scalar.activation(x2T[:], misc[:, bank_of("x2T"), 0:GT], ACT.Copy).then_inc(misc_read[0], 1)
                if prv is not None:
                    misc_wait_read(act, "x2T", it)
                    nc.scalar.activation(x2_high[:, bass.ds(prv * GT, GT)], x2T[:], ACT.Copy).then_inc(x2high_done, 1)
                if cur is not None:
                    act.wait_ge(pv_done[1], cur * GB + GB)
                    nc.scalar.activation(headsT[:], heads[:], ACT.Copy).then_inc(headsT_done, 1)
                    misc_wait_full(act, "merged", it)
                    nc.scalar.activation(mergedT[:], misc[:, bank_of("merged"), 0:GT], ACT.Copy).then_inc(misc_read[0], 1)
            loop(act, body)

            act.wait_ge(g_dve, 2)
            nc.scalar.activation(g_exp[:], g_exp[:], ACT.Exp).then_inc(g_act, 1)
            nc.scalar.activation(g_thr[:], logits[:, :, E], ACT.Exp, scale=-1.0).then_inc(g_act, 1)
            act.wait_ge(wT_zeroed, 1)
            for q in range(4):
                act.wait_ge(g_full, q + 1)
                nc.scalar.activation(expert_wT[0:3 * E, 1024 * q:1024 * (q + 1)], ps_wT[0:3 * E, q, :], ACT.Copy).then_inc(g_copied, 1)

            wait_spare_loads(act)

            def body_b(g):
                for j in range(CH):
                    e = j // FC
                    act.wait_ge(h_full, g * CH + (j + 1))
                    wait_count(act, low2_done, g * CH + (j - HBUF + 1))
                    nc.scalar.activation(h_sb[:, j % HBUF, :], ps_h[:, j % 4, :], ACT.Gelu_apprx_tanh,
                                         bias=b1_sb[:, j:j + 1]).then_inc(h_done, 1)
                    if j % FC == 2:
                        act.wait_ge(wrow_full, g * E + (e + 1))
                        wait_count(act, weighted_done, g * E + (e - 1))
                        nc.scalar.activation(w_row[:, e % 2, :], ps_w[:], ACT.Copy).then_inc(wrow_done, 1)
            loop_b(act, body_b)

        @block.vector
        def _(dve):
            def ln1(lo, hi):
                for t in range(lo, hi):
                    nc.vector.bn_stats(stats[:, t, :], x_all[:, t, :]).then_inc(ln1_stats, 1)
                for t in range(lo, hi):
                    dve.wait_ge(ln1_stats, t + 1)
                    nc.vector.bn_aggr(mean_var[:, t, :], stats[:, t, :]).then_inc(ln1_aggr, 1)
            nc.vector.memset(q_masked[:].bitcast(F32), 0.0).then_inc(pad_done, 1)
            nc.vector.memset(k_masked[:].bitcast(F32), 0.0).then_inc(pad_done, 1)
            dve.wait_ge(x_in, 16)
            ln1(0, GB)
            dve.wait_ge(wts_in, N_WTS)
            nc.vector.tensor_tensor(bqk_low[:], bqk[:], low_rows[:], ALU.mult).then_inc(bias_low_done, 1)
            dve.wait_ge(qk_w_done, 4)
            nc.vector.tensor_tensor(wqk_low[:], wqk_raw, wqk_high[:].bitcast(F32), ALU.subtract).then_inc(qk_w_done, 1)
            nc.vector.tensor_tensor(wv_low[:], wv_raw, wv_high[:].bitcast(F32), ALU.subtract).then_inc(qk_w_done, 1)

            def max_half(cur, b, u):
                dve.wait_ge(scores_full[u], fill_N(cur, b))
                nc.vector.tensor_reduce(neg_max[:, b, 8 * u:8 * u + 8],
                                        scores[:, 2 * u:2 * u + 2, :].rearrange("p a (r k) -> p (a r) k", k=S),
                                        AX.X, ALU.max, negate=True).then_inc(scores_read[u], 1)

            def body(prv, cur, nxt):
                it = (prv, cur, nxt)

                def stacks(i):
                    k = bank_of(f"p{i}{i + 1}")
                    dve.wait_ge(part_done, nxt * (2 * SLABS) + (i + 2))
                    for j in (i, i + 1):
                        dst = (k_stack if j < SLABS else q_stack)[:, j % SLABS, :]
                        ins = nc.vector.scalar_tensor_tensor(dst, misc[:, k, (j - i) * GT:(j - i + 1) * GT], bqk[:, j:j + 1],
                                                             part[:, j % 4, :].bitcast(F32), ALU.add, ALU.subtract)
                    ins.then_inc(misc_read[k], 1)

                if nxt is not None:
                    misc_wait_full(dve, "ctxT", it)
                    dve.wait_ge(high_done, 2 * nxt + 1)
                    nc.vector.tensor_tensor(ctxT_low[:], misc[:, bank_of("ctxT"), 0:GT], ctxT_high[:].bitcast(F32), ALU.subtract).then_inc(misc_read[1], 1)
                    dve.wait_ge(high_done, 2 * nxt + 2)
                    nc.vector.tensor_tensor(xT_low[:], misc[:, bank_of("xT"), 0:GT], xT_high[:].bitcast(F32), ALU.subtract).then_inc(misc_read[2], 1)
                if prv is not None:
                    if nxt is None:
                        dve.wait_ge(misc_read[2], fills("wo", (NG - 2, NG - 1, None)) - (1 if cur is not None else 0))
                    for b in range(GB):
                        nc.vector.bn_stats(stats2[:, b, :], x_all[:, bass.ds(prv * GB + b, 1), :].rearrange("p b d -> p (b d)")).then_inc(stats2_done, 1)
                    second_norm_var(prv)
                if nxt is not None:
                    wait_count(dve, km_in, nxt * (ROWS * 16))
                    wait_count(dve, kcur_in, nxt * 16)
                    wait_count(dve, qm_in, nxt * (ROWS * 16))
                    stacks(0)
                    stacks(2)
                    stacks(4)
                if prv is not None:
                    for b in range(GB):
                        dve.wait_ge(rstd2_done, prv + 1)
                        settle(dve)
                        t = bass.ds(prv * GB + b, 1)
                        nc.vector.tensor_scalar(x2n[:, b, :], x_all[:, t, :].rearrange("p b d -> p (b d)"),
                                                mean_var2[:, b, 0:1], rstd2[:, b:b + 1], ALU.subtract, ALU.mult).then_inc(x2n_done, 1)
                if nxt is not None:
                    stacks(6)
                    if cur is None:
                        dve.wait_ge(x_rest_in, 16)
                        ln1(GB, B)
                        dve.wait_ge(const_pool, 4)
                if prv is not None:
                    misc_wait_full(dve, "gate", it)
                    nc.vector.tensor_tensor(logits[:, bass.ds(prv * GB, GB), :],
                                            misc[:, bank_of("gate"), 0:GB * NGATE].rearrange("p (b e) -> p b e", e=NGATE),
                                            bg_row[:].unsqueeze(1).to_broadcast([P, GB, NGATE]), ALU.add).then_inc(misc_read[0], 1)
                if nxt is not None:
                    max_half(cur, 0, 0)
                    misc_wait_full(dve, "v", it)
                    if cur is not None:
                        dve.wait_ge(pv_done[1], cur * GB + GB)
                    for b in range(GB):
                        dst = bass.AP(v_pad, b * H * 32, [[GB * H * 32, P], [64, H // 2], [48, 2], [1, HD]])
                        ins = nc.vector.tensor_tensor(dst, misc[:, bank_of("v"), b * D:(b + 1) * D].rearrange("p (h o d) -> p h o d", o=2, d=HD),
                                                      bv_row[:].rearrange("p (h o d) -> p h o d", o=2, d=HD), ALU.add)
                    ins.then_inc(misc_read[2], 1)
                    max_half(cur, 0, 1)
                if cur is not None:
                    misc_wait_full(dve, "heads", it)
                    hv = misc[:, bank_of("heads"), :].rearrange("p (bh c) -> p bh c", c=16)
                    nc.vector.reciprocal(sums_r[:].unsqueeze(2), hv[:, :, 8:9]).then_inc(recip_done, 1)
                    dve.wait_ge(recip_done, cur + 1)
                    nc.vector.tensor_tensor(merged[:], hv[:, :, 0:HD], sums_r[:].unsqueeze(2).to_broadcast([P, GB * H, HD]),
                                            ALU.mult).then_inc(misc_read[1], 1)
                if nxt is not None:
                    max_half(cur, 1, 0)
                if cur is not None:
                    misc_wait_full(dve, "wo", it)
                    dve.wait_ge(biased_done, cur + 1)
                    nc.vector.scalar_tensor_tensor(x_all[:, bass.ds(cur * GB, GB), :].rearrange("p b d -> p (b d)"),
                                                   misc[:, bank_of("wo"), 0:GT], tanh_g[:, 0:1], x_biased[:].rearrange("p b d -> p (b d)"),
                                                   ALU.mult, ALU.add).then_inc(misc_read[2], 1)
                if nxt is not None:
                    max_half(cur, 1, 1)
                    for u in range(2):
                        dve.wait_ge(scores_read[u], fill_N(cur, GB - 1))
                    nc.vector.tensor_copy(max_parts[:, :, 0:H], neg_max[:]).then_inc(maxhigh_done, 1)
                    dve.wait_ge(maxhigh_done, nxt + 1)
                    nc.vector.tensor_tensor(max_parts[:, :, H:2 * H], neg_max[:], max_parts[:, :, 0:H].bitcast(F32), ALU.subtract).then_inc(max_done, 1)

            def second_norm_var(prv):
                for b in range(GB):
                    dve.wait_ge(stats2_done, prv * GB + (b + 1))
                    settle(dve)
                    nc.vector.bn_aggr(mean_var2[:, b, :], stats2[:, b, :]).then_inc(aggr2_done, 1)
                dve.wait_ge(aggr2_done, prv * GB + GB)
                nc.vector.tensor_scalar(rstd2[:], mean_var2[:, :, 1], EPS, None, ALU.add).then_inc(var2_done, 1)
            loop(dve, body)

            steps = [0]

            def step(ins):
                steps[0] += 1
                ins.then_inc(g_dve, 1)
                dve.wait_ge(g_dve, steps[0])
            wide = [P, B, E]
            V = nc.vector
            misc_wait_read(dve, "gate", (NG - 1, None, None))
            step(V.tensor_reduce(g_max[:], logits[:, :, 0:E], AX.X, ALU.max))
            step(V.tensor_tensor(g_exp[:], logits[:, :, 0:E], g_max[:].unsqueeze(2).to_broadcast(wide), ALU.subtract))
            dve.wait_ge(g_act, 2)
            step(V.tensor_reduce(g_sum[:], g_exp[:], AX.X, ALU.add))
            step(V.reciprocal(g_sum[:], g_sum[:]))
            step(V.tensor_tensor(g_exp[:], g_exp[:], g_sum[:].unsqueeze(2).to_broadcast(wide), ALU.mult))
            step(V.tensor_scalar(g_thr[:], g_thr[:], 1.0 / MAX_THRESHOLD, 1.0 / MAX_THRESHOLD, ALU.mult, ALU.add))
            step(V.reciprocal(g_thr[:], g_thr[:]))
            step(V.tensor_tensor(g_exp[:], g_exp[:], g_thr[:].unsqueeze(2).to_broadcast(wide), ALU.subtract))
            step(V.tensor_scalar(g_exp[:], g_exp[:], 0.0, None, ALU.max))
            step(V.tensor_reduce(g_sum[:], g_exp[:], AX.X, ALU.add))
            step(V.tensor_scalar(g_max[:], g_sum[:], 0.0, None, ALU.is_equal))
            step(V.tensor_tensor(g_sum[:], g_sum[:], g_max[:], ALU.add))
            step(V.reciprocal(g_sum[:], g_sum[:]))
            step(V.tensor_scalar(g_sum[:], g_sum[:], tanh_g[:, 1:2], None, ALU.mult))
            step(V.tensor_tensor(g_exp[:], g_exp[:], g_sum[:].unsqueeze(2).to_broadcast(wide), ALU.mult))
            for j in range(3):
                step(V.tensor_copy(w_parts[:, :, E * j:E * (j + 1)], g_exp[:]))
                if j < 2:
                    step(V.tensor_tensor(g_exp[:], g_exp[:], w_parts[:, :, E * j:E * (j + 1)], ALU.subtract))

            wait_spare_loads(dve)

            def finish(g):
                dve.wait_ge(t_full, g + 1)
                wait_count(dve, y_stored, g * 16)
                V.tensor_tensor(y_out[:], ps_t[:], x_all[:, bass.ds(g * TPB, TPB), :], ALU.add).then_inc(t_read, 1)

            def combine(g, e):
                dve.wait_ge(w2_done, g * CH + FC * (e + 1))
                dve.wait_ge(wrow_done, g * E + (e + 1))
                if e >= 2:
                    wait_count(dve, added, g * (E - 1) + (e - 2))
                elif e == 1:
                    wait_count(dve, added, g * (E - 1))
                else:
                    wait_count(dve, t_full, g)
                dst = yT[:] if e == 0 else weighted[:, e % 2, :]
                V.scalar_tensor_tensor(dst, ps_y[:, e % 2, :], b2_sb[:, e:e + 1], w_row[:, e % 2, :],
                                       ALU.add, ALU.mult).then_inc(weighted_done, 1)

            def body_b(g):
                def high(j):
                    dve.wait_ge(h_done, g * CH + (j + 1))
                    wait_count(dve, w2_done, g * CH + (j - HBUF + 1))
                    V.tensor_copy(h_high[:, j % HBUF, :], h_sb[:, j % HBUF, :]).then_inc(high2_done, 1)

                def low(j):
                    dve.wait_ge(high2_done, g * CH + (j + 1))
                    V.tensor_tensor(h_low[:, j % HBUF, :], h_sb[:, j % HBUF, :], h_high[:, j % HBUF, :].bitcast(F32),
                                    ALU.subtract).then_inc(low2_done, 1)

                high(0)
                for j in range(CH):
                    if j + 1 < CH:
                        high(j + 1)
                    low(j)
                    if j == 2 and not (isinstance(g, int) and g == 0):
                        finish(g - 1)
                    if j >= FC + LAG and j % FC == 0:
                        combine(g, (j - LAG) // FC - 1)
                for e in range((CH - LAG) // FC - 1, E):
                    combine(g, e)
            loop_b(dve, body_b)
            finish(NB - 1)

        @block.tensor
        def _(pe):
            mm = nc.tensor.matmul

            def body(prv, cur, nxt):
                it = (prv, cur, nxt)

                def turn(what, src, rows=P):
                    k = bank_of(what)
                    misc_wait_free(pe, what, it)
                    for b in range(GB):
                        ins = nc.tensor.transpose(misc[0:rows, k, b * S:(b + 1) * S], src(b), ident[:])
                    ins.then_inc(misc_full[k], 1)

                def project(i):
                    what = f"p{i}{i + 1}"
                    k = bank_of(what)
                    misc_wait_free(pe, what, it)
                    src_h, src_l = (ctxT_high, ctxT_low) if i < SLABS else (xT_high, xT_low)
                    for j in (i, i + 1):
                        at = (j + SLABS) % (2 * SLABS) * P
                        cols = slice(at, at + P)
                        dst = misc[:, k, (j - i) * GT:(j - i + 1) * GT]
                        mm(dst, wqk_high[:, cols], src_h[:], start=True, stop=False)
                        mm(dst, wqk_high[:, cols], src_l[:], start=False, stop=False)
                        ins = mm(dst, wqk_low[:, cols], src_h[:], start=False, stop=True)
                    ins.then_inc(misc_full[k], 1)

                if nxt is not None:
                    pe.wait_ge(ctx_in, nxt * 16 + 16)
                    turn("ctxT", lambda b: ctx_sb[:, b, :])
                    pe.wait_ge(xn_done, nxt * GB + GB)
                    turn("xT", lambda b: xn[:, b, :])
                    if cur is None:
                        pe.wait_ge(qk_w_done, 6)
                if cur is not None:
                    pe.wait_ge(max_done, cur + 1)
                    turn("max", lambda b: max_parts[:, b, :].bitcast(F32), 2 * H)
                if nxt is not None:
                    misc_wait_read(pe, "ctxT", it)
                    project(0)
                    project(2)
                    misc_wait_read(pe, "xT", it)
                    project(4)
                if cur is not None:
                    pe.wait_ge(kcur_in, cur * 16 + 16)
                    pe.wait_ge(qm_in, cur * (ROWS * 16) + ROWS * 16)
                    pe.wait_ge(max_in, cur * 32 + 32)
                    pe.wait_ge(maskcur_done, cur + 1)
                    transposed(cur, 0, 0)
                    transposed(cur, 0, 1)
                if nxt is not None:
                    project(6)
                if cur is not None:
                    transposed(cur, 1, 0)
                    values(cur, 0, 0)
                    transposed(cur, 1, 1)
                    values(cur, 0, 1)
                if prv is not None:
                    pe.wait_ge(x2n_done, prv * GB + GB)
                    turn("x2T", lambda b: x2n[:, b, :])
                if nxt is not None:
                    misc_wait_free(pe, "v", it)
                    for b in range(GB):
                        dst = misc[:, bank_of("v"), b * D:(b + 1) * D]
                        h_, l_ = ctxT_high[:, b * S:(b + 1) * S], ctxT_low[:, b * S:(b + 1) * S]
                        mm(dst, h_, wv_high[:], start=True, stop=False)
                        mm(dst, l_, wv_high[:], start=False, stop=False)
                        ins = mm(dst, h_, wv_low[:], start=False, stop=True)
                    ins.then_inc(misc_full[2], 1)
                if cur is not None:
                    values(cur, 1, 0)
                if nxt is not None:
                    natural(it, 0, 0)
                if cur is not None:
                    values(cur, 1, 1)
                if prv is not None:
                    misc_wait_read(pe, "x2T", it)
                    misc_wait_free(pe, "gate", it)
                    for b in range(GB):
                        ins = mm(misc[:, bank_of("gate"), b * NGATE:(b + 1) * NGATE], x2T[:, b * S:(b + 1) * S], wg_sb[:], start=True, stop=True)
                    ins.then_inc(misc_full[0], 1)
                if nxt is not None:
                    natural(it, 0, 1)
                if cur is not None:
                    misc_wait_free(pe, "heads", it)
                    pe.wait_ge(headsT_done, cur + 1)
                    for b in range(GB):
                        for k in range(2):
                            ins = nc.tensor.transpose(misc[:, bank_of("heads"), (2 * b + k) * P:(2 * b + k + 1) * P],
                                                      headsT[:, b, k * P:(k + 1) * P], ident[:])
                    ins.then_inc(misc_full[1], 1)
                if nxt is not None:
                    natural(it, 1, 0)
                if cur is not None:
                    misc_wait_read(pe, "heads", it)
                    turn("merged", lambda b: merged[:, b * H:(b + 1) * H, :].rearrange("p h d -> p (h d)"))
                if nxt is not None:
                    natural(it, 1, 1)
                if cur is not None:
                    misc_wait_read(pe, "merged", it)
                    misc_wait_free(pe, "wo", it)
                    for b in range(GB):
                        ins = mm(misc[:, bank_of("wo"), b * D:(b + 1) * D], mergedT[:, b * S:(b + 1) * S], wo_sb[:], start=True, stop=True)
                    ins.then_inc(misc_full[2], 1)

            def transposed(cur, b, u):
                pe.wait_ge(scores_read[u], fill_T(cur, b) - 1)
                for s in (2 * u, 2 * u + 1):
                    dst = scores[:, s, :].rearrange("p (r q) -> p r q", r=ROWS)
                    mm(dst, k_cur[:, s, b * S:(b + 1) * S], q_masked[:, s, :, b * S:(b + 1) * S], start=True, stop=False)
                    ins = mm(dst, mask_cur[:, b, :], masked_ident[:].unsqueeze(1).to_broadcast([P, ROWS, P]),
                             start=False, stop=True)
                ins.then_inc(scores_full[u], 1)

            def values(cur, b, k):
                pe.wait_ge(scores_read[k], fill_T(cur, b))
                if b == 0 and k == 0:
                    wait_count(pe, headsT_done, cur)
                for o in range(2):
                    for t in range(4):
                        hh = 2 * t + o
                        ins = mm(heads[32 * t:32 * t + 32, b, k * P:(k + 1) * P], v_pad[:, b, 8 * k + hh, :],
                                 probs[:, k, hh * S:(hh + 1) * S], start=(o == 0), stop=(o == 1))
                ins.then_inc(pv_done[k], 1)

            def natural(it, b, u):
                prv, cur, nxt = it
                if b == 0 and u == 0:
                    pe.wait_ge(km_in, nxt * (ROWS * 16) + ROWS * 16)
                    misc_wait_read(pe, "p45", it)
                    misc_wait_read(pe, "p67", it)
                    pe.wait_ge(masknxt_done, nxt + 1)
                wait_count(pe, scores_read[u], fill_N(cur, b) - 1)
                for s in (2 * u, 2 * u + 1):
                    dst = scores[:, s, :].rearrange("p (r k) -> p r k", r=ROWS)
                    mm(dst, q_stack[:, s, b * S:(b + 1) * S], k_masked[:, s, :, b * S:(b + 1) * S], start=True, stop=False)
                    ins = mm(dst, masked_ident[:], mask_nxt[:, b, :].unsqueeze(1).to_broadcast([P, ROWS, S]), start=False, stop=True)
                ins.then_inc(scores_full[u], 1)

            pe.wait_ge(wts_in, N_WTS)
            pe.wait_ge(const_act, 2)
            loop(pe, body)

            pe.wait_ge(g_dve, 20)
            for q in range(4):
                for k in range(8):
                    ins = nc.tensor.transpose(ps_wT[0:3 * E, q, k * P:(k + 1) * P], w_parts[:, 8 * q + k, :], ident_b[:])
                ins.then_inc(g_full, 1)
            pe.wait_ge(g_copied, 4)
            pe.wait_ge(sel_done, 1)
            pe.wait_ge(wsplit_done, NW)
            pe.wait_ge(x2low_done, NG)
            pe.wait_ge(x2high_done, NG)

            def second(g, j):
                e, f = divmod(j, FC)
                if f == 0:
                    wait_count(pe, weighted_done, g * E + (e - 1) if e >= 2 else g * E)
                pe.wait_ge(high2_done, g * CH + (j + 1))
                pe.wait_ge(low2_done, g * CH + (j + 1))
                dst = ps_y[:, e % 2, :]
                cols = slice(f * P, (f + 1) * P)
                mm(dst, w_high[:, E + e, cols], h_high[:, j % HBUF, :], start=(f == 0), stop=False)
                mm(dst, w_high[:, E + e, cols], h_low[:, j % HBUF, :], start=False, stop=False)
                mm(dst, w_low[:, E + e, cols], h_high[:, j % HBUF, :], start=False, stop=(f == FC - 1)).then_inc(w2_done, 1)

            def untranspose(g):
                pe.wait_ge(added, (g + 1) * (E - 1))
                wait_count(pe, t_read, g)
                for t in range(TPB):
                    ins = nc.tensor.transpose(ps_t[:, t, :], yT[:, t * P:(t + 1) * P], ident[:])
                ins.then_inc(t_full, 1)

            def body_b(g):
                for j in range(CH):
                    e, f = divmod(j, FC)
                    wait_count(pe, h_done, g * CH + (j - 3) if j >= 4 else g * CH)
                    dst = ps_h[:, j % 4, :]
                    cols = slice(f * P, (f + 1) * P)
                    xh, xl = x2_high[:, bass.ds(g * BT, BT)], x2_low[:, bass.ds(g * BT, BT)]
                    mm(dst, w_high[:, e, cols], xh, start=True, stop=False)
                    mm(dst, w_high[:, e, cols], xl, start=False, stop=False)
                    mm(dst, w_low[:, e, cols], xh, start=False, stop=True).then_inc(h_full, 1)
                    if f == 1:
                        wait_count(pe, wrow_done, g * E + e)
                        mm(ps_w[:], sel[:, e, :], expert_wT[:, bass.ds(g * BT, BT)], start=True, stop=True).then_inc(wrow_full, 1)
                    if j == 2 and not (isinstance(g, int) and g == 0):
                        untranspose(g - 1)
                    if j >= LAG:
                        second(g, j - LAG)
                for j in range(CH - LAG, CH):
                    second(g, j)
            loop_b(pe, body_b)
            untranspose(NB - 1)


def kernel(**inputs):
    import numpy as np
    import concourse.bacc as bacc
    from concourse.bass_utils import run_bass_kernel_spmd

    v = {k: np.ascontiguousarray(x) for k, x in inputs.items()}

    def stack(w, axis_last):
        w = w.reshape(SLABS, ROWS, HD, axis_last)
        out = np.zeros((SLABS, ROWS, COMBOS, HD, axis_last), w.dtype)
        for c in range(3):
            out[:, :, c] = w
        return out.reshape(SLABS * P, axis_last)

    bq = stack(v["L0_xattn_bq"].reshape(D, 1), 1).reshape(SLABS, ROWS, COMBOS, HD)
    bk = stack(v["L0_xattn_bk"].reshape(D, 1), 1).reshape(SLABS, ROWS, COMBOS, HD)
    bk[:, 0, 3, 0:2] = 1.0
    low = np.zeros((2, SLABS, ROWS, COMBOS, HD), np.float32)
    low[0, :, :, 1] = 1.0
    low[1, :, :, 2] = 1.0
    sel = np.zeros((P, E, P), np.uint8)
    for e in range(E):
        for j in range(3):
            sel[E * j + e, e, :] = 1
    w2 = v["L0_ffn_W2"].reshape(E, FC, P, D).transpose(0, 2, 1, 3).reshape(E, P, FC * D)
    arrays = {
        "x": v["x"].reshape(TOK, D),
        "ctx": v["ctx_1024"].reshape(TOK, D),
        "mask": v["mask_BxSxS2_bk1"].view(np.int32),
        "wqk": np.concatenate([stack(v["L0_xattn_Wq"], D).T, stack(v["L0_xattn_Wk"], D).T], 1),
        "bqk": np.concatenate([bk.reshape(SLABS, P), bq.reshape(SLABS, P)], 0).T,
        "low_rows": low.reshape(2 * SLABS, P).T,
        "wvT": v["L0_xattn_Wv"].T,
        "woT": v["L0_xattn_Wo"].T,
        "bv": v["L0_xattn_bv"].reshape(1, D),
        "bo": v["L0_xattn_bo"].reshape(1, D),
        "g": np.concatenate([v["g_xattn"], v["g_ffn"]]).reshape(1, 2),
        "w_ffn": np.concatenate([v["L0_ffn_W1"], w2, w2[0:1]], 0),
        "b1": v["L0_ffn_b1"].reshape(CH, P).T,
        "b2": v["L0_ffn_b2"].T,
        "wg": np.concatenate([v["L0_ffn_Wg"], v["L0_ffn_Wt"]], 1),
        "bg": np.concatenate([v["L0_ffn_bg"], v["L0_ffn_bt"]]).reshape(1, NGATE),
        "ident": np.eye(P, dtype=np.float32),
        "sel": sel.reshape(P, E * P).view(np.int32),
    }
    arrays["ctx"] = np.concatenate([arrays["ctx"], arrays["ctx"][0:GT]], 0)
    arrays["mask"] = np.concatenate([arrays["mask"], arrays["mask"][0:GB]], 0)
    nc = bacc.Bacc("TRN2", target_bir_lowering=False, num_devices=1)
    feed, aps = {}, {}
    for name, arr in arrays.items():
        arr = np.ascontiguousarray(arr)
        feed[f"in_{name}"] = arr
        aps[name] = nc.dram_tensor(f"in_{name}", arr.shape, mybir.dt.from_np(arr.dtype), kind="ExternalInput").ap()
    aps["out"] = nc.dram_tensor("out_y", (TOK, D), F32, kind="ExternalOutput").ap()
    gated_block(nc, aps)
    r = run_bass_kernel_spmd(nc, [feed], core_ids=[0])
    return r.results[0]["out_y"].reshape(B, S, D)
```

```python
from contextlib import ExitStack

import concourse.bass as bass
from concourse import mybir

F32 = mybir.dt.float32
F32R = mybir.dt.float32r
BF16 = mybir.dt.bfloat16
U8 = mybir.dt.uint8
I32 = mybir.dt.int32
ALU = mybir.AluOpType
ACT = mybir.ActivationFunctionType
AX = mybir.AxisListType

P = 128
B, S, D = 32, 128, 128
H, HD = 16, 8
E, FF = 8, 512
TOK = B * S
GB = 2
GT = GB * S
NG = B // GB
SLABS, ROWS = 4, 4
COMBOS = 4
FC = FF // P
CH = E * FC
BT = 512
NB = TOK // BT
TPB = BT // P
LAG = 4
HBUF = 8
NGATE = E + 1
EPS = 1e-5
SCALE = float(HD) ** -0.5
MASKED = -(2.0 ** 126)
MAX_THRESHOLD = 0.125
NW = 2 * E

BANKS = [["merged", "p23", "x2T", "gate"],
         ["p01", "p67", "heads"],
         ["inputs", "wo", "p45", "v"]]
OF_CUR = {"heads"}
OF_PRV = {"merged", "wo", "x2T", "gate"}


def bank_of(what):
    return [what in order for order in BANKS].index(True)


def fills(what, it):
    prv, cur, nxt = it
    order = BANKS[bank_of(what)]
    present = [w for w in order if (prv if w in OF_PRV else cur if w in OF_CUR else nxt) is not None]
    n_prv = sum(w in OF_PRV for w in order)
    n_cur = sum(w in OF_CUR for w in order)
    n_nxt = len(order) - n_prv - n_cur
    at = present.index(what) + 1
    if cur is None and prv is None:
        return at
    if cur is None:
        return n_nxt * NG + n_cur * NG + n_prv * (NG - 1) + at
    if nxt is None:
        return n_nxt * NG + n_cur * (NG - 1) + n_prv * (NG - 2) + at
    if prv is None:
        return n_nxt + at
    return cur * len(order) + (n_nxt - n_prv + at)


def gated_block(nc, a):
    ctx = ExitStack()
    phase_a = ExitStack()
    phase_b = ExitStack()
    with ctx:
        def sb(name, shape, dt, stack=ctx):
            return stack.enter_context(nc.sbuf_tensor(name, shape, dt))

        def sem(name):
            return ctx.enter_context(nc.semaphore(name))

        x_all = sb("x_all", [P, B, D], F32)
        x2_high = sb("x2_high", [P, TOK], F32R)
        x2_low = sb("x2_low", [P, TOK], F32R)
        w_high = sb("w_high", [P, NW, 512], F32R)
        w_low = sb("w_low", [P, NW, 512], F32R)
        b1_sb = sb("b1_sb", [P, CH], F32)
        b2_sb = sb("b2_sb", [P, E], F32)
        ident = sb("ident_sb", [P, P], F32)
        ident_b = sb("ident_b", [P, P], BF16)
        gates = sb("gates", [P, 2], F32)
        tanh_g = sb("tanh_g", [P, 2], F32)

        def sa(name, shape, dt):
            return sb(name, shape, dt, phase_a)
        k_masked = sa("k_masked", [P, SLABS, ROWS, GT], F32R)
        q_masked = sa("q_masked", [P, SLABS, ROWS, GT], F32R)
        k_stack = sa("k_stack", [P, SLABS, GT], F32R)
        q_stack = sa("q_stack", [P, SLABS, GT], F32R)
        k_cur = sa("k_cur", [P, SLABS, GT], F32R)
        probs = sa("probs", [P, 2, 8 * S], F32)
        v_pad = sa("v_pad", [P, GB, H, 32], F32)
        ctx_sb = sa("ctx_sb", [P, GB, D], F32)
        xn = sa("xn", [P, GB, D], F32)
        inT_high = sa("inT_high", [P, 2 * GT], F32R)
        inT_low = sa("inT_low", [P, 2 * GT], F32R)
        part = sa("part", [P, 4, GT], F32R)
        mask_words = sa("mask_words", [P, GB, S // 4], I32)
        mask_nxt = sa("mask_nxt", [P, GB, S], BF16)
        mask_cur = sa("mask_cur", [P, GB, S], BF16)
        masked_ident = sa("masked_ident", [P, P], BF16)
        wqk_raw = probs[:, 0, 0:2 * SLABS * P]
        wv_raw = probs[:, 1, 0:P]
        wqk_high = sa("wqk_high", [P, 2 * SLABS * P], F32R)
        wqk_low = sa("wqk_low", [P, 2 * SLABS * P], F32R)
        wv_high = sa("wv_high", [P, P], F32R)
        wv_low = sa("wv_low", [P, P], F32R)
        wo_sb = sa("wo_sb", [P, P], F32)
        bqk = sa("bqk", [P, 2 * SLABS], F32)
        bqk_low = sa("bqk_low", [P, 2 * SLABS], F32)
        low_rows = sa("low_rows_sb", [P, 2 * SLABS], F32)
        bv_row = sa("bv_row", [P, P], F32)
        bo_row = sa("bo_row", [P, P], F32)
        bg_row = sa("bg_row", [P, NGATE], F32)
        wg_sb = sa("wg_sb", [P, NGATE], F32)
        stats = sa("stats", [P, B, 6], F32)
        mean_var = sa("mean_var", [P, B, 2], F32)
        rstd = sa("rstd", [P, B], F32)
        shift = sa("shift", [P, B], F32)
        power = sa("power", [P, B], F32)
        neg_max = sa("neg_max", [P, GB, H], F32)
        max_parts = sa("max_parts", [P, GB, 2 * H], F32R)
        maxT = sa("maxT", [2 * H, GT], F32R)
        headsT = sa("headsT", [P, GB, 2 * P], F32)
        sums_r = sa("sums_r", [P, GB * H], F32)
        merged = sa("merged", [P, GB * H, HD], F32)
        mergedT = sa("mergedT", [P, GT], F32)
        x_biased = sa("x_biased", [P, GB, D], F32)
        stats2 = sa("stats2", [P, GB, 6], F32)
        mean_var2 = sa("mean_var2", [P, GB, 2], F32)
        rstd2 = sa("rstd2", [P, GB], F32)
        x2n = sa("x2n", [P, GB, D], F32)
        x2T = sa("x2T_sb", [P, GT], F32)
        w_raw = sa("w_raw", [P, 512], F32)
        logits = sa("logits", [P, B, NGATE], F32)
        g_max = sa("g_max", [P, B], F32)
        g_exp = sa("g_exp", [P, B, E], F32)
        g_sum = sa("g_sum", [P, B], F32)
        g_thr = sa("g_thr", [P, B], F32)
        w_parts = sa("w_parts", [P, B, 3 * E], BF16)
        phase_a.close()

        def sbb(name, shape, dt):
            return sb(name, shape, dt, phase_b)
        expert_wT = sbb("expert_wT", [P, TOK], BF16)
        sel_words = sbb("sel_words", [P, E * P // 4], I32)
        sel = sbb("sel_b", [P, E, P], BF16)
        h_sb = sbb("h_sb", [P, HBUF, BT], F32)
        h_high = sbb("h_high", [P, HBUF, BT], F32R)
        h_low = sbb("h_low", [P, HBUF, BT], F32R)
        w_row = sbb("w_row", [P, 2, BT], F32)
        weighted = sbb("weighted", [P, 2, BT], F32)
        yT = sbb("yT", [P, BT], F32)
        y_out = sbb("y_out", [P, TPB, D], F32)
        phase_b.close()

        psum_a = ExitStack()
        scores = psum_a.enter_context(nc.psum_tensor("scores", [P, 4, 512], F32))
        misc = psum_a.enter_context(nc.psum_tensor("misc", [P, 3, 512], F32))
        heads = psum_a.enter_context(nc.psum_tensor("heads", [P, GB, GT], F32))
        psum_a.close()
        psum_b = ExitStack()
        ps_h = psum_b.enter_context(nc.psum_tensor("ps_h", [P, 4, BT], F32))
        ps_w = psum_b.enter_context(nc.psum_tensor("ps_w", [P, BT], F32))
        ps_t = psum_b.enter_context(nc.psum_tensor("ps_t", [P, TPB, D], F32))
        ps_y = psum_b.enter_context(nc.psum_tensor("ps_y", [P, 2, BT], F32))
        psum_b.close()
        psum_g = ExitStack()
        ps_wT = psum_g.enter_context(nc.psum_tensor("ps_wT", [P, 4, 1024], BF16))
        psum_g.close()

        x_in = sem("x_in")
        x_rest_in = sem("x_rest_in")
        waited = sem("waited")
        wts_early_in = sem("wts_early_in")
        wts_in = sem("wts_in")
        ctx_in = sem("ctx_in")
        mask_in = sem("mask_in")
        w_in = sem("w_in")
        sel_in = sem("sel_in")
        const_pool = sem("const_pool")
        const_act = sem("const_act")
        bias_low_done = sem("bias_low_done")
        qk_w_done = sem("qk_w_done")
        ln1_stats = sem("ln1_stats")
        ln1_aggr = sem("ln1_aggr")
        ln1_pool = sem("ln1_pool")
        ln1_done = sem("ln1_done")
        pad_done = sem("pad_done")
        xn_scaled = sem("xn_scaled")
        xn_done = sem("xn_done")
        high_done = sem("high_done")
        part_done = sem("part_done")
        misc_full = [sem("misc0_full"), sem("misc1_full"), sem("misc2_full")]
        misc_read = [sem("misc0_read"), sem("misc1_read"), sem("misc2_read")]
        scoresT_full = [sem("scoresT0_full"), sem("scoresT1_full")]
        scoresT_read = [sem("scoresT0_read"), sem("scoresT1_read")]
        scoresN_full = [sem("scoresN0_full"), sem("scoresN1_full")]
        scoresN_read = [sem("scoresN0_read"), sem("scoresN1_read")]
        probs_done = [sem("probs0_done"), sem("probs1_done")]
        pv_done = [sem("pv0_done"), sem("pv1_done")]
        headsT_done = sem("headsT_done")
        km_in = sem("km_in")
        kcur_in = sem("kcur_in")
        qm_in = sem("qm_in")
        max_in = sem("max_in")
        maxhigh_done = sem("maxhigh_done")
        max_done = sem("max_done")
        max_full = sem("max_full")
        maxT_done = sem("maxT_done")
        recip_done = sem("recip_done")
        biased_done = sem("biased_done")
        x1_done = sem("x1_done")
        stats2_done = sem("stats2_done")
        aggr2_done = sem("aggr2_done")
        var2_done = sem("var2_done")
        rstd2_done = sem("rstd2_done")
        x2n_done = sem("x2n_done")
        x2T_done = sem("x2T_done")
        x2high_done = sem("x2high_done")
        x2low_done = sem("x2low_done")
        masknxt_done = sem("masknxt_done")
        maskcur_done = sem("maskcur_done")
        wsplit_high = sem("wsplit_high")
        wsplit_done = sem("wsplit_done")
        g_dve = sem("g_dve")
        g_act = sem("g_act")
        g_full = sem("g_full")
        wT_zeroed = sem("wT_zeroed")
        g_copied = sem("g_copied")
        sel_done = sem("sel_done")
        h_full = sem("h_full")
        h_done = sem("h_done")
        high2_done = sem("high2_done")
        low2_done = sem("low2_done")
        w2_done = sem("w2_done")
        wrow_full = sem("wrow_full")
        wrow_done = sem("wrow_done")
        weighted_done = sem("weighted_done")
        added = sem("added")
        t_full = sem("t_full")
        t_read = sem("t_read")
        y_stored = sem("y_stored")

        block = ctx.enter_context(nc.Block())

        N_WTS_EARLY = 7 * 16
        N_WTS = 7 * 16

        def settle(eng):
            eng.sem_inc(waited, 1)

        def misc_wait_full(eng, what, it):
            k = bank_of(what)
            eng.wait_ge(misc_full[k], fills(what, it))

        def misc_wait_read(eng, what, it):
            k = bank_of(what)
            eng.wait_ge(misc_read[k], fills(what, it))

        def misc_wait_free(eng, what, it):
            k = bank_of(what)
            n = fills(what, it)
            if not (isinstance(n, int) and n == 1):
                eng.wait_ge(misc_read[k], n - 1)

        def last_heads(it):
            prv, cur, nxt = it
            if nxt is None and cur is None:
                return fills("heads", (NG - 2, NG - 1, None))
            return fills("p01" if nxt is not None else "heads", it) - 1

        def wait_count(eng, s, n):
            if not (isinstance(n, int) and n <= 0):
                eng.wait_ge(s, n)

        def fill_of(group, b, s):
            return group * (GB * SLABS // 2) + (b * (SLABS // 2) + s // 2 + 1)

        def loop(eng, body):
            body(None, None, 0)
            body(None, 0, 1)
            body(0, 1, 2)
            with eng.Fori(2, NG - 1) as cur:
                body(cur - 1, cur, cur + 1)
            body(NG - 2, NG - 1, None)
            body(NG - 1, None, None)

        def wait_spare_loads(eng):
            eng.wait_ge(ctx_in, 16 * (NG + 1))
            eng.wait_ge(mask_in, 16 * (NG + 1))
            eng.wait_ge(w_in, 16 * (NG + 1))

        def loop_b(eng, body):
            body(0)
            body(1)
            with eng.Fori(2, NB) as g:
                body(g)

        @block.sync
        def _(sp):
            ctx_v = a["ctx"].rearrange("(g b p) d -> g p b d", p=P, b=GB)
            mask_v = a["mask"].rearrange("(g b) q k -> g q b k", b=GB)
            sp.dma_start(x_all[:, 0:2 * GB, :], a["x"][0:2 * GB * S, :].rearrange("(b p) d -> p b d", p=P)).then_inc(x_in, 16)
            sp.dma_start(ident[:], a["ident"]).then_inc(wts_early_in, 16)
            sp.dma_start(ctx_sb[:], ctx_v[0]).then_inc(ctx_in, 16)
            sp.dma_start(wqk_raw[:, SLABS * P:], a["wqk"][:, SLABS * P:]).then_inc(wts_early_in, 16)
            sp.dma_start(wqk_raw[:, 0:SLABS * P], a["wqk"][:, 0:SLABS * P]).then_inc(wts_early_in, 16)
            sp.dma_start(bqk[:], a["bqk"]).then_inc(wts_early_in, 16)
            sp.dma_start(low_rows[:], a["low_rows"]).then_inc(wts_early_in, 16)
            sp.dma_start(wv_raw, a["wvT"]).then_inc(wts_early_in, 16)
            sp.dma_start(gates[:], a["g"].partition_broadcast(P)).then_inc(wts_early_in, 16)
            sp.dma_start(mask_words[:], mask_v[0]).then_inc(mask_in, 16)
            sp.dma_start(bv_row[:], a["bv"].partition_broadcast(P)).then_inc(wts_in, 16)
            sp.dma_start(bo_row[:], a["bo"].partition_broadcast(P)).then_inc(wts_in, 16)
            sp.dma_start(wo_sb[:], a["woT"]).then_inc(wts_in, 16)
            sp.dma_start(wg_sb[:], a["wg"]).then_inc(wts_in, 16)
            sp.dma_start(bg_row[:], a["bg"].partition_broadcast(P)).then_inc(wts_in, 16)
            sp.dma_start(b1_sb[:], a["b1"]).then_inc(wts_in, 16)
            sp.dma_start(b2_sb[:], a["b2"]).then_inc(wts_in, 16)
            sp.dma_start(w_raw[:], a["w_ffn"][0]).then_inc(w_in, 16)
            sp.dma_start(x_all[:, 2 * GB:, :], a["x"][2 * GB * S:, :].rearrange("(b p) d -> p b d", p=P)).then_inc(x_rest_in, 16)

            def body(prv, cur, nxt):
                it = (prv, cur, nxt)
                if nxt is not None:
                    dyn = prv is not None and not isinstance(prv, int)
                    ahead = cur + 2 if dyn else nxt + 1
                    at = bass.ds(ahead, 1) if dyn else ahead
                    misc_wait_full(sp, "inputs", it)
                    settle(sp)
                    sp.dma_start(ctx_sb[:], ctx_v[at]).then_inc(ctx_in, 16)
                if cur is not None:
                    sp.wait_ge(maxT_done, cur + 1)
                    settle(sp)
                    sp.dma_start(q_masked[24:26, :, :, :].rearrange("p s r q -> p (s r) q").bitcast(F32),
                                 maxT[:].bitcast(F32)).then_inc(max_in, 16)
                if nxt is not None:
                    misc_wait_read(sp, "p01", it)
                    settle(sp)
                    misc_wait_read(sp, "p23", it)
                    settle(sp)
                    if cur is not None:
                        sp.wait_ge(scoresN_full[1], fill_of(cur, GB - 1, SLABS - 1))
                        settle(sp)
                    else:
                        sp.wait_ge(pad_done, 2)
                    for r in range(ROWS):
                        rows = slice(32 * r, 32 * r + 32)
                        sp.dma_start(k_masked[rows, :, r, :].bitcast(F32), k_stack[rows, :, :].bitcast(F32)).then_inc(km_in, 16)
                    sp.wait_ge(wsplit_done, nxt + 1)
                    settle(sp)
                    sp.dma_start(w_raw[:], a["w_ffn"][at]).then_inc(w_in, 16)
                    misc_wait_read(sp, "p45", it)
                    settle(sp)
                    misc_wait_read(sp, "p67", it)
                    settle(sp)
                    if cur is not None:
                        sp.wait_ge(scoresT_full[1], fill_of(cur, GB - 1, SLABS - 1))
                        settle(sp)
                    sp.dma_start(k_cur[:].bitcast(F32), k_stack[:].bitcast(F32)).then_inc(kcur_in, 16)
                    for r in range(ROWS):
                        rows = slice(32 * r, 32 * r + 24)
                        sp.dma_start(q_masked[rows, :, r, :].bitcast(F32), q_stack[rows, :, :].bitcast(F32)).then_inc(qm_in, 16)
                    sp.wait_ge(maskcur_done, nxt + 1)
                    settle(sp)
                    sp.dma_start(mask_words[:], mask_v[at]).then_inc(mask_in, 16)
            loop(sp, body)
            out_v = a["out"].rearrange("(g t p) d -> g p t d", p=P, t=TPB)
            with sp.Fori(0, NB) as g:
                sp.wait_ge(t_read, g + 1)
                settle(sp)
                sp.dma_start(out_v[g], y_out[:]).then_inc(y_stored, 16)
            sp.wait_ge(y_stored, 16 * NB)

        @block.gpsimd
        def _(pool):
            nc.gpsimd.memset(power[:], -0.5).then_inc(const_pool, 1)
            nc.gpsimd.memset(v_pad[:], 0.0).then_inc(const_pool, 1)
            pool.wait_ge(const_pool, 2)
            vv = v_pad[:].rearrange("p b (hh o) c -> p (b hh) o c", o=2)
            nc.gpsimd.memset(vv[:, :, 0, 8:16], 1.0).then_inc(const_pool, 1)
            nc.gpsimd.memset(vv[:, :, 1, 24:32], 1.0).then_inc(const_pool, 1)
            nc.gpsimd.memset(k_masked[:].bitcast(F32), 0.0).then_inc(pad_done, 1)

            def first_norm(n, lo, hi):
                pool.wait_ge(ln1_aggr, hi)
                nc.gpsimd.tensor_scalar(rstd[:, lo:hi], mean_var[:, lo:hi, 1], EPS, 1.0, ALU.add, ALU.mult).then_inc(ln1_pool, 1)
                pool.wait_ge(ln1_pool, 4 * n + 1)
                nc.gpsimd.tensor_tensor(rstd[:, lo:hi], rstd[:, lo:hi], power[:, lo:hi], ALU.pow).then_inc(ln1_pool, 1)
                pool.wait_ge(ln1_pool, 4 * n + 2)
                nc.gpsimd.tensor_tensor(shift[:, lo:hi], mean_var[:, lo:hi, 0], rstd[:, lo:hi], ALU.mult).then_inc(ln1_pool, 1)
                pool.wait_ge(ln1_pool, 4 * n + 3)
                nc.gpsimd.tensor_scalar(shift[:, lo:hi], shift[:, lo:hi], -1.0, 0.0, ALU.mult, ALU.add).then_inc(ln1_pool, 1)
                pool.wait_ge(ln1_pool, 4 * n + 4)
            first_norm(0, 0, 2 * GB)
            for b in range(GB):
                nc.gpsimd.tensor_scalar(xn[:, b, :], x_all[:, b, :], rstd[:, b:b + 1], shift[:, b:b + 1],
                                        ALU.mult, ALU.add).then_inc(xn_done, 1)
            pool.wait_ge(wts_in, N_WTS)
            pool.wait_ge(qk_w_done, 1)
            nc.gpsimd.tensor_scalar(bo_row[:], bo_row[:], tanh_g[:, 0:1], 0.0, ALU.mult, ALU.add).then_inc(const_pool, 1)

            def body(prv, cur, nxt):
                if nxt is not None:
                    if cur is not None:
                        last = {None: (None, None, 0), 0: (None, 0, 1)}.get(prv if prv is None or isinstance(prv, int) else "x")
                        k = bank_of("inputs")
                        pool.wait_ge(misc_full[k], fills("inputs", last) if last else (cur - 1) * len(BANKS[k]) + fills("inputs", (0, 0, 0)))
                        settle(pool)
                        ts = bass.ds(cur * GB + GB, GB)
                        nc.gpsimd.tensor_tensor(xn[:], x_all[:, ts, :], rstd[:, ts].unsqueeze(2).to_broadcast([P, GB, D]),
                                                ALU.mult).then_inc(xn_scaled, 1)
                        pool.wait_ge(xn_scaled, cur + 1)
                        settle(pool)
                        nc.gpsimd.tensor_tensor(xn[:], xn[:], shift[:, ts].unsqueeze(2).to_broadcast([P, GB, D]),
                                                ALU.add).then_inc(xn_done, GB)
                if cur is not None:
                    if prv is not None:
                        misc_wait_read(pool, "wo", (prv, cur, nxt))
                        settle(pool)
                    nc.gpsimd.tensor_tensor(x_biased[:], x_all[:, bass.ds(cur * GB, GB), :],
                                            bo_row[:].unsqueeze(1).to_broadcast([P, GB, D]), ALU.add).then_inc(biased_done, 1)
                if prv is not None:
                    pool.wait_ge(var2_done, prv + 1)
                    settle(pool)
                    nc.gpsimd.tensor_tensor(rstd2[:], rstd2[:], power[:, 0:GB], ALU.pow).then_inc(rstd2_done, 1)
                if nxt is not None:
                    if cur is not None:
                        pool.wait_ge(scoresN_full[1], fill_of(cur, GB - 1, SLABS - 1))
                        settle(pool)
                    pool.wait_ge(mask_in, 16 * nxt + 16)
                    settle(pool)
                    nc.gpsimd.tensor_copy(mask_nxt[:], mask_words[:].bitcast(U8)).then_inc(masknxt_done, 1)
                    pool.wait_ge(w_in, 16 * nxt + 16)
                    settle(pool)
                    nc.gpsimd.tensor_copy(w_high[:, bass.ds(nxt, 1), :], w_raw[:]).then_inc(wsplit_high, 1)
                    pool.wait_ge(wsplit_high, nxt + 1)
                    settle(pool)
                    nc.gpsimd.tensor_tensor(w_low[:, bass.ds(nxt, 1), :], w_raw[:],
                                            w_high[:, bass.ds(nxt, 1), :].bitcast(F32), ALU.subtract).then_inc(wsplit_done, 1)
                    if cur is not None:
                        pool.wait_ge(scoresT_full[1], fill_of(cur, GB - 1, SLABS - 1))
                        settle(pool)
                    nc.gpsimd.tensor_copy(mask_cur[:], mask_words[:].bitcast(U8)).then_inc(maskcur_done, 1)
                if cur is not None and prv is None:
                    first_norm(1, 2 * GB, B)
                if prv is not None:
                    pool.wait_ge(x2high_done, prv + 1)
                    settle(pool)
                    nc.gpsimd.tensor_tensor(x2_low[:, bass.ds(prv * GT, GT)], x2T[:],
                                            x2_high[:, bass.ds(prv * GT, GT)].bitcast(F32), ALU.subtract).then_inc(x2low_done, 1)
            pool.wait_ge(const_pool, 5)
            loop(pool, body)

            wait_spare_loads(pool)
            pool.wait_ge(x2high_done, NG)
            nc.gpsimd.memset(expert_wT[:], 0.0).then_inc(wT_zeroed, 1)
            nc.gpsimd.dma_start(sel_words[:], a["sel"]).then_inc(sel_in, 16)
            pool.wait_ge(sel_in, 16)
            nc.gpsimd.tensor_copy(sel[:].rearrange("p e m -> p (e m)"), sel_words[:].bitcast(U8)).then_inc(sel_done, 1)

            def body_b(g):
                for e in range(1, E):
                    pool.wait_ge(weighted_done, g * E + (e + 1))
                    if e > 1:
                        pool.wait_ge(added, g * (E - 1) + (e - 1))
                    nc.gpsimd.tensor_tensor(yT[:], yT[:], weighted[:, e % 2, :], ALU.add).then_inc(added, 1)
            loop_b(pool, body_b)

        @block.scalar
        def _(act):
            act.wait_ge(wts_early_in, N_WTS_EARLY)
            nc.scalar.activation(tanh_g[:], gates[:], ACT.Tanh).then_inc(qk_w_done, 1)
            nc.scalar.activation(wqk_high[:, SLABS * P:], wqk_raw[:, SLABS * P:], ACT.Copy).then_inc(qk_w_done, 1)
            nc.scalar.activation(wqk_high[:, 0:SLABS * P], wqk_raw[:, 0:SLABS * P], ACT.Copy).then_inc(qk_w_done, 1)
            nc.scalar.activation(wv_high[:], wv_raw, ACT.Copy).then_inc(qk_w_done, 1)
            nc.scalar.activation(ident_b[:], ident[:], ACT.Copy).then_inc(const_act, 1)
            nc.scalar.activation(masked_ident[:], ident[:], ACT.Copy, scale=MASKED).then_inc(const_act, 1)

            def exp_slab(cur, b, s):
                act.wait_ge(scoresT_full[s % 2], fill_of(cur, b, s))
                wait_count(act, pv_done[s // 2], cur * GB + b)
                nc.scalar.activation(probs[:, s // 2, (s % 2) * 4 * S:(s % 2 + 1) * 4 * S], scores[:, s % 2, :],
                                     ACT.Exp, scale=SCALE).then_inc(scoresT_read[s % 2], 1)

            def body(prv, cur, nxt):
                it = (prv, cur, nxt)

                def parts(i):
                    what = f"p{i}{i + 1}"
                    misc_wait_full(act, what, it)
                    if i >= SLABS:
                        misc_wait_read(act, f"p{i - 4}{i - 3}", it)
                    for k in range(2):
                        nc.scalar.activation(part[:, (i + k) % 4, :], misc[:, bank_of(what), k * GT:(k + 1) * GT], ACT.Identity,
                                             scale=low_rows[:, i + k:i + k + 1],
                                             bias=bqk_low[:, i + k:i + k + 1]).then_inc(part_done, 1)

                if nxt is not None:
                    misc_wait_full(act, "inputs", it)
                    nc.scalar.activation(inT_high[:], misc[:, bank_of("inputs"), :], ACT.Copy).then_inc(high_done, 1)
                if prv is not None:
                    misc_wait_full(act, "merged", it)
                    nc.scalar.activation(mergedT[:], misc[:, bank_of("merged"), 0:GT], ACT.Copy).then_inc(misc_read[0], 1)
                if nxt is not None:
                    if cur is None:
                        act.wait_ge(bias_low_done, 1)
                    parts(0)
                if cur is not None:
                    act.wait_ge(max_full, cur + 1)
                    wait_count(act, max_in, cur * 16)
                    nc.scalar.activation(maxT[:], heads[0:2 * H, 0, :], ACT.Copy).then_inc(maxT_done, 1)
                if nxt is not None:
                    parts(2)
                if nxt is not None:
                    parts(4)
                    parts(6)
                if cur is not None:
                    for b in range(GB):
                        for s in range(SLABS):
                            exp_slab(cur, b, s)
                if prv is not None:
                    misc_wait_full(act, "x2T", it)
                    wait_count(act, x2low_done, prv)
                    nc.scalar.activation(x2T[:], misc[:, bank_of("x2T"), 0:GT], ACT.Copy).then_inc(misc_read[0], 1)
                if prv is not None:
                    misc_wait_read(act, "x2T", it)
                    nc.scalar.activation(x2_high[:, bass.ds(prv * GT, GT)], x2T[:], ACT.Copy).then_inc(x2high_done, 1)
                if cur is not None:
                    act.wait_ge(pv_done[1], cur * GB + GB)
                    nc.scalar.activation(headsT[:], heads[:], ACT.Copy).then_inc(headsT_done, 1)
            loop(act, body)

            act.wait_ge(g_dve, 2)
            nc.scalar.activation(g_exp[:], g_exp[:], ACT.Exp).then_inc(g_act, 1)
            nc.scalar.activation(g_thr[:], logits[:, :, E], ACT.Exp, scale=-1.0).then_inc(g_act, 1)
            act.wait_ge(wT_zeroed, 1)
            for q in range(4):
                act.wait_ge(g_full, q + 1)
                nc.scalar.activation(expert_wT[0:3 * E, 1024 * q:1024 * (q + 1)], ps_wT[0:3 * E, q, :], ACT.Copy).then_inc(g_copied, 1)

            wait_spare_loads(act)
            act.wait_ge(wts_in, N_WTS)

            def body_b(g):
                for j in range(CH):
                    e = j // FC
                    act.wait_ge(h_full, g * CH + (j + 1))
                    wait_count(act, low2_done, g * CH + (j - HBUF + 1))
                    nc.scalar.activation(h_sb[:, j % HBUF, :], ps_h[:, j % 4, :], ACT.Gelu_apprx_tanh,
                                         bias=b1_sb[:, j:j + 1]).then_inc(h_done, 1)
                    if j % FC == 2:
                        act.wait_ge(wrow_full, g * E + (e + 1))
                        wait_count(act, weighted_done, g * E + (e - 1))
                        nc.scalar.activation(w_row[:, e % 2, :], ps_w[:], ACT.Copy).then_inc(wrow_done, 1)
            loop_b(act, body_b)

        @block.vector
        def _(dve):
            def ln1(lo, hi):
                for t in range(lo, hi):
                    nc.vector.bn_stats(stats[:, t, :], x_all[:, t, :]).then_inc(ln1_stats, 1)
                for t in range(lo, hi):
                    dve.wait_ge(ln1_stats, t + 1)
                    nc.vector.bn_aggr(mean_var[:, t, :], stats[:, t, :]).then_inc(ln1_aggr, 1)
            dve.wait_ge(x_in, 16)
            ln1(0, 2 * GB)
            nc.vector.memset(q_masked[:].bitcast(F32), 0.0).then_inc(pad_done, 1)
            dve.wait_ge(wts_early_in, N_WTS_EARLY)
            nc.vector.tensor_tensor(bqk_low[:], bqk[:], low_rows[:], ALU.mult).then_inc(bias_low_done, 1)
            dve.wait_ge(qk_w_done, 4)
            nc.vector.tensor_tensor(wqk_low[:], wqk_raw, wqk_high[:].bitcast(F32), ALU.subtract).then_inc(qk_w_done, 1)
            nc.vector.tensor_tensor(wv_low[:], wv_raw, wv_high[:].bitcast(F32), ALU.subtract).then_inc(qk_w_done, 1)

            def max_slab(group, b, s):
                dve.wait_ge(scoresN_full[s % 2], fill_of(group, b, s))
                nc.vector.tensor_reduce(neg_max[:, b, ROWS * s:ROWS * s + ROWS],
                                        scores[:, 2 + s % 2, :].rearrange("p (r k) -> p r k", k=S),
                                        AX.X, ALU.max, negate=True).then_inc(scoresN_read[s % 2], 1)

            def body(prv, cur, nxt):
                it = (prv, cur, nxt)

                def stacks(i):
                    k = bank_of(f"p{i}{i + 1}")
                    dve.wait_ge(part_done, nxt * (2 * SLABS) + (i + 2))
                    for j in (i, i + 1):
                        dst = (k_stack if j < SLABS else q_stack)[:, j % SLABS, :]
                        ins = nc.vector.scalar_tensor_tensor(dst, misc[:, k, (j - i) * GT:(j - i + 1) * GT], bqk[:, j:j + 1],
                                                             part[:, j % 4, :].bitcast(F32), ALU.add, ALU.subtract)
                    ins.then_inc(misc_read[k], 1)

                if nxt is not None:
                    dve.wait_ge(high_done, nxt + 1)
                    nc.vector.tensor_tensor(inT_low[:], misc[:, bank_of("inputs"), :], inT_high[:].bitcast(F32),
                                            ALU.subtract).then_inc(misc_read[2], 1)
                if cur is not None:
                    max_slab(cur, 1, 2)
                    max_slab(cur, 1, 3)
                    for u in range(2):
                        dve.wait_ge(scoresN_read[u], fill_of(cur, GB - 1, SLABS - 1))
                    nc.vector.tensor_copy(max_parts[:, :, 0:H], neg_max[:]).then_inc(maxhigh_done, 1)
                    dve.wait_ge(maxhigh_done, cur + 1)
                    nc.vector.tensor_tensor(max_parts[:, :, H:2 * H], neg_max[:], max_parts[:, :, 0:H].bitcast(F32), ALU.subtract).then_inc(max_done, 1)
                if prv is not None:
                    misc_wait_full(dve, "wo", it)
                    dve.wait_ge(biased_done, prv + 1)
                    nc.vector.scalar_tensor_tensor(x_all[:, bass.ds(prv * GB, GB), :].rearrange("p b d -> p (b d)"),
                                                   misc[:, bank_of("wo"), 0:GT], tanh_g[:, 0:1], x_biased[:].rearrange("p b d -> p (b d)"),
                                                   ALU.mult, ALU.add).then_inc(misc_read[2], 1)
                if nxt is not None:
                    wait_count(dve, km_in, nxt * (ROWS * 16))
                    wait_count(dve, kcur_in, nxt * 16)
                    wait_count(dve, qm_in, nxt * (ROWS * 16))
                    stacks(0)
                if prv is not None:
                    misc_wait_read(dve, "wo", it)
                    settle(dve)
                    for b in range(GB):
                        nc.vector.bn_stats(stats2[:, b, :], x_all[:, bass.ds(prv * GB + b, 1), :].rearrange("p b d -> p (b d)")).then_inc(stats2_done, 1)
                if nxt is not None:
                    stacks(2)
                if prv is not None:
                    second_norm_var(prv)
                if nxt is not None:
                    stacks(4)
                if prv is not None:
                    for b in range(GB):
                        dve.wait_ge(rstd2_done, prv + 1)
                        settle(dve)
                        t = bass.ds(prv * GB + b, 1)
                        nc.vector.tensor_scalar(x2n[:, b, :], x_all[:, t, :].rearrange("p b d -> p (b d)"),
                                                mean_var2[:, b, 0:1], rstd2[:, b:b + 1], ALU.subtract, ALU.mult).then_inc(x2n_done, 1)
                if nxt is not None:
                    stacks(6)
                    if cur is None:
                        dve.wait_ge(wts_in, N_WTS)
                        dve.wait_ge(const_pool, 4)
                    elif prv is None:
                        dve.wait_ge(x_rest_in, 16)
                        ln1(2 * GB, B)
                if nxt is not None:
                    for s in range(SLABS):
                        max_slab(nxt, 0, s)
                if prv is not None:
                    misc_wait_full(dve, "gate", it)
                    nc.vector.tensor_tensor(logits[:, bass.ds(prv * GB, GB), :],
                                            misc[:, bank_of("gate"), 0:GB * NGATE].rearrange("p (b e) -> p b e", e=NGATE),
                                            bg_row[:].unsqueeze(1).to_broadcast([P, GB, NGATE]), ALU.add).then_inc(misc_read[0], 1)
                if nxt is not None:
                    misc_wait_full(dve, "v", it)
                    if cur is not None:
                        dve.wait_ge(pv_done[1], cur * GB + GB)
                    for b in range(GB):
                        dst = bass.AP(v_pad, b * H * 32, [[GB * H * 32, P], [64, H // 2], [48, 2], [1, HD]])
                        ins = nc.vector.tensor_tensor(dst, misc[:, bank_of("v"), b * D:(b + 1) * D].rearrange("p (h o d) -> p h o d", o=2, d=HD),
                                                      bv_row[:].rearrange("p (h o d) -> p h o d", o=2, d=HD), ALU.add)
                    ins.then_inc(misc_read[2], 1)
                    max_slab(nxt, 1, 0)
                    max_slab(nxt, 1, 1)
                if cur is not None:
                    misc_wait_full(dve, "heads", it)
                    hv = misc[:, bank_of("heads"), :].rearrange("p (bh c) -> p bh c", c=16)
                    nc.vector.reciprocal(sums_r[:].unsqueeze(2), hv[:, :, 8:9]).then_inc(recip_done, 1)
                    dve.wait_ge(recip_done, cur + 1)
                    nc.vector.tensor_tensor(merged[:], hv[:, :, 0:HD], sums_r[:].unsqueeze(2).to_broadcast([P, GB * H, HD]),
                                            ALU.mult).then_inc(misc_read[1], 1)
            def second_norm_var(prv):
                for b in range(GB):
                    dve.wait_ge(stats2_done, prv * GB + (b + 1))
                    settle(dve)
                    nc.vector.bn_aggr(mean_var2[:, b, :], stats2[:, b, :]).then_inc(aggr2_done, 1)
                dve.wait_ge(aggr2_done, prv * GB + GB)
                nc.vector.tensor_scalar(rstd2[:], mean_var2[:, :, 1], EPS, None, ALU.add).then_inc(var2_done, 1)
            loop(dve, body)

            steps = [0]

            def step(ins):
                steps[0] += 1
                ins.then_inc(g_dve, 1)
                dve.wait_ge(g_dve, steps[0])
            wide = [P, B, E]
            V = nc.vector
            misc_wait_read(dve, "gate", (NG - 1, None, None))
            step(V.tensor_reduce(g_max[:], logits[:, :, 0:E], AX.X, ALU.max))
            step(V.tensor_tensor(g_exp[:], logits[:, :, 0:E], g_max[:].unsqueeze(2).to_broadcast(wide), ALU.subtract))
            dve.wait_ge(g_act, 2)
            step(V.tensor_reduce(g_sum[:], g_exp[:], AX.X, ALU.add))
            step(V.reciprocal(g_sum[:], g_sum[:]))
            step(V.tensor_tensor(g_exp[:], g_exp[:], g_sum[:].unsqueeze(2).to_broadcast(wide), ALU.mult))
            step(V.tensor_scalar(g_thr[:], g_thr[:], 1.0 / MAX_THRESHOLD, 1.0 / MAX_THRESHOLD, ALU.mult, ALU.add))
            step(V.reciprocal(g_thr[:], g_thr[:]))
            step(V.tensor_tensor(g_exp[:], g_exp[:], g_thr[:].unsqueeze(2).to_broadcast(wide), ALU.subtract))
            step(V.tensor_scalar(g_exp[:], g_exp[:], 0.0, None, ALU.max))
            step(V.tensor_reduce(g_sum[:], g_exp[:], AX.X, ALU.add))
            step(V.tensor_scalar(g_max[:], g_sum[:], 0.0, None, ALU.is_equal))
            step(V.tensor_tensor(g_sum[:], g_sum[:], g_max[:], ALU.add))
            step(V.reciprocal(g_sum[:], g_sum[:]))
            step(V.tensor_scalar(g_sum[:], g_sum[:], tanh_g[:, 1:2], None, ALU.mult))
            step(V.tensor_tensor(g_exp[:], g_exp[:], g_sum[:].unsqueeze(2).to_broadcast(wide), ALU.mult))
            for j in range(3):
                step(V.tensor_copy(w_parts[:, :, E * j:E * (j + 1)], g_exp[:]))
                if j < 2:
                    step(V.tensor_tensor(g_exp[:], g_exp[:], w_parts[:, :, E * j:E * (j + 1)], ALU.subtract))

            wait_spare_loads(dve)

            def finish(g):
                dve.wait_ge(t_full, g + 1)
                wait_count(dve, y_stored, g * 16)
                V.tensor_tensor(y_out[:], ps_t[:], x_all[:, bass.ds(g * TPB, TPB), :], ALU.add).then_inc(t_read, 1)

            def combine(g, e):
                dve.wait_ge(w2_done, g * CH + FC * (e + 1))
                dve.wait_ge(wrow_done, g * E + (e + 1))
                if e >= 2:
                    wait_count(dve, added, g * (E - 1) + (e - 2))
                elif e == 1:
                    wait_count(dve, added, g * (E - 1))
                else:
                    wait_count(dve, t_full, g)
                dst = yT[:] if e == 0 else weighted[:, e % 2, :]
                V.scalar_tensor_tensor(dst, ps_y[:, e % 2, :], b2_sb[:, e:e + 1], w_row[:, e % 2, :],
                                       ALU.add, ALU.mult).then_inc(weighted_done, 1)

            def body_b(g):
                def high(j):
                    dve.wait_ge(h_done, g * CH + (j + 1))
                    wait_count(dve, w2_done, g * CH + (j - HBUF + 1))
                    V.tensor_copy(h_high[:, j % HBUF, :], h_sb[:, j % HBUF, :]).then_inc(high2_done, 1)

                def low(j):
                    dve.wait_ge(high2_done, g * CH + (j + 1))
                    V.tensor_tensor(h_low[:, j % HBUF, :], h_sb[:, j % HBUF, :], h_high[:, j % HBUF, :].bitcast(F32),
                                    ALU.subtract).then_inc(low2_done, 1)

                high(0)
                for j in range(CH):
                    if j + 1 < CH:
                        high(j + 1)
                    low(j)
                    if j == 2 and not (isinstance(g, int) and g == 0):
                        finish(g - 1)
                    if j >= FC + LAG and j % FC == 0:
                        combine(g, (j - LAG) // FC - 1)
                for e in range((CH - LAG) // FC - 1, E):
                    combine(g, e)
            loop_b(dve, body_b)
            finish(NB - 1)

        @block.tensor
        def _(pe):
            mm = nc.tensor.matmul

            def body(prv, cur, nxt):
                it = (prv, cur, nxt)

                def turn(what, src, n=GB):
                    k = bank_of(what)
                    misc_wait_free(pe, what, it)
                    for b in range(n):
                        ins = nc.tensor.transpose(misc[:, k, b * S:(b + 1) * S], src(b), ident[:])
                    ins.then_inc(misc_full[k], 1)

                def project(i):
                    what = f"p{i}{i + 1}"
                    k = bank_of(what)
                    misc_wait_free(pe, what, it)
                    at = 0 if i < SLABS else GT
                    src_h, src_l = inT_high[:, at:at + GT], inT_low[:, at:at + GT]
                    for j in (i, i + 1):
                        at = (j + SLABS) % (2 * SLABS) * P
                        cols = slice(at, at + P)
                        dst = misc[:, k, (j - i) * GT:(j - i + 1) * GT]
                        mm(dst, wqk_high[:, cols], src_h, start=True, stop=False)
                        mm(dst, wqk_high[:, cols], src_l, start=False, stop=False)
                        ins = mm(dst, wqk_low[:, cols], src_h, start=False, stop=True)
                    ins.then_inc(misc_full[k], 1)

                if nxt is not None:
                    pe.wait_ge(ctx_in, nxt * 16 + 16)
                    pe.wait_ge(xn_done, nxt * GB + GB)
                    turn("inputs", lambda b: ctx_sb[:, b, :] if b < GB else xn[:, b - GB, :], 2 * GB)
                    if cur is None:
                        pe.wait_ge(qk_w_done, 6)
                if cur is not None:
                    natural(cur, 1, 2)
                    natural(cur, 1, 3)
                if prv is not None:
                    pe.wait_ge(misc_read[1], last_heads(it))
                    turn("merged", lambda b: merged[:, b * H:(b + 1) * H, :].rearrange("p h d -> p (h d)"))
                if nxt is not None:
                    misc_wait_read(pe, "inputs", it)
                    project(0)
                if prv is not None:
                    misc_wait_read(pe, "merged", it)
                    misc_wait_free(pe, "wo", it)
                    for b in range(GB):
                        ins = mm(misc[:, bank_of("wo"), b * D:(b + 1) * D], mergedT[:, b * S:(b + 1) * S], wo_sb[:], start=True, stop=True)
                    ins.then_inc(misc_full[2], 1)
                if cur is not None:
                    pe.wait_ge(max_done, cur + 1)
                    wait_count(pe, headsT_done, cur)
                    for b in range(GB):
                        ins = nc.tensor.transpose(heads[0:2 * H, 0, b * S:(b + 1) * S], max_parts[:, b, :].bitcast(F32), ident[:])
                    ins.then_inc(max_full, 1)
                if nxt is not None:
                    project(2)
                    project(4)
                    project(6)
                    if cur is None:
                        pe.wait_ge(wts_in, N_WTS)
                if cur is not None:
                    pe.wait_ge(kcur_in, cur * 16 + 16)
                    pe.wait_ge(qm_in, cur * (ROWS * 16) + ROWS * 16)
                    pe.wait_ge(max_in, cur * 16 + 16)
                    pe.wait_ge(maskcur_done, cur + 1)
                    for s in range(SLABS):
                        transposed(cur, 0, s)
                    values(cur, 0, 0)
                    transposed(cur, 1, 0)
                    transposed(cur, 1, 1)
                if prv is not None:
                    pe.wait_ge(x2n_done, prv * GB + GB)
                    turn("x2T", lambda b: x2n[:, b, :])
                if cur is not None:
                    values(cur, 0, 1)
                if nxt is not None:
                    pe.wait_ge(km_in, nxt * (ROWS * 16) + ROWS * 16)
                    misc_wait_read(pe, "p45", it)
                    misc_wait_read(pe, "p67", it)
                    pe.wait_ge(masknxt_done, nxt + 1)
                    natural(nxt, 0, 0)
                if cur is not None:
                    transposed(cur, 1, 2)
                if nxt is not None:
                    natural(nxt, 0, 1)
                if cur is not None:
                    transposed(cur, 1, 3)
                if nxt is not None:
                    natural(nxt, 0, 2)
                if cur is not None:
                    values(cur, 1, 0)
                if nxt is not None:
                    natural(nxt, 0, 3)
                if prv is not None:
                    misc_wait_read(pe, "x2T", it)
                    misc_wait_free(pe, "gate", it)
                    for b in range(GB):
                        ins = mm(misc[:, bank_of("gate"), b * NGATE:(b + 1) * NGATE], x2T[:, b * S:(b + 1) * S], wg_sb[:], start=True, stop=True)
                    ins.then_inc(misc_full[0], 1)
                if nxt is not None:
                    misc_wait_free(pe, "v", it)
                    for b in range(GB):
                        dst = misc[:, bank_of("v"), b * D:(b + 1) * D]
                        h_, l_ = inT_high[:, b * S:(b + 1) * S], inT_low[:, b * S:(b + 1) * S]
                        mm(dst, h_, wv_high[:], start=True, stop=False)
                        mm(dst, l_, wv_high[:], start=False, stop=False)
                        ins = mm(dst, h_, wv_low[:], start=False, stop=True)
                    ins.then_inc(misc_full[2], 1)
                if cur is not None:
                    values(cur, 1, 1)
                if nxt is not None:
                    natural(nxt, 1, 0)
                    natural(nxt, 1, 1)
                if cur is not None:
                    misc_wait_free(pe, "heads", it)
                    pe.wait_ge(headsT_done, cur + 1)
                    for b in range(GB):
                        for k in range(2):
                            ins = nc.tensor.transpose(misc[:, bank_of("heads"), (2 * b + k) * P:(2 * b + k + 1) * P],
                                                      headsT[:, b, k * P:(k + 1) * P], ident[:])
                    ins.then_inc(misc_full[1], 1)

            def transposed(cur, b, s):
                wait_count(pe, scoresT_read[s % 2], fill_of(cur, b, s) - 1)
                dst = scores[:, s % 2, :].rearrange("p (r q) -> p r q", r=ROWS)
                mm(dst, k_cur[:, s, b * S:(b + 1) * S], q_masked[:, s, :, b * S:(b + 1) * S], start=True, stop=False)
                mm(dst, mask_cur[:, b, :], masked_ident[:].unsqueeze(1).to_broadcast([P, ROWS, P]),
                   start=False, stop=True).then_inc(scoresT_full[s % 2], 1)

            def natural(nxt, b, s):
                wait_count(pe, scoresN_read[s % 2], fill_of(nxt, b, s) - 1)
                dst = scores[:, 2 + s % 2, :].rearrange("p (r k) -> p r k", r=ROWS)
                mm(dst, q_stack[:, s, b * S:(b + 1) * S], k_masked[:, s, :, b * S:(b + 1) * S], start=True, stop=False)
                mm(dst, masked_ident[:], mask_nxt[:, b, :].unsqueeze(1).to_broadcast([P, ROWS, S]),
                   start=False, stop=True).then_inc(scoresN_full[s % 2], 1)

            def values(cur, b, k):
                for s in (2 * k, 2 * k + 1):
                    pe.wait_ge(scoresT_read[s % 2], fill_of(cur, b, s))
                if b == 0 and k == 0:
                    wait_count(pe, headsT_done, cur)
                for o in range(2):
                    for t in range(4):
                        hh = 2 * t + o
                        ins = mm(heads[32 * t:32 * t + 32, b, k * P:(k + 1) * P], v_pad[:, b, 8 * k + hh, :],
                                 probs[:, k, hh * S:(hh + 1) * S], start=(o == 0), stop=(o == 1))
                ins.then_inc(pv_done[k], 1)

            pe.wait_ge(wts_early_in, N_WTS_EARLY)
            pe.wait_ge(const_act, 2)
            loop(pe, body)

            pe.wait_ge(g_dve, 20)
            for q in range(4):
                for k in range(8):
                    ins = nc.tensor.transpose(ps_wT[0:3 * E, q, k * P:(k + 1) * P], w_parts[:, 8 * q + k, :], ident_b[:])
                ins.then_inc(g_full, 1)
            pe.wait_ge(g_copied, 4)
            pe.wait_ge(sel_done, 1)
            pe.wait_ge(wsplit_done, NW)
            pe.wait_ge(x2low_done, NG)
            pe.wait_ge(x2high_done, NG)

            def second(g, j):
                e, f = divmod(j, FC)
                if f == 0:
                    wait_count(pe, weighted_done, g * E + (e - 1) if e >= 2 else g * E)
                pe.wait_ge(high2_done, g * CH + (j + 1))
                pe.wait_ge(low2_done, g * CH + (j + 1))
                dst = ps_y[:, e % 2, :]
                cols = slice(f * P, (f + 1) * P)
                mm(dst, w_high[:, E + e, cols], h_high[:, j % HBUF, :], start=(f == 0), stop=False)
                mm(dst, w_high[:, E + e, cols], h_low[:, j % HBUF, :], start=False, stop=False)
                mm(dst, w_low[:, E + e, cols], h_high[:, j % HBUF, :], start=False, stop=(f == FC - 1)).then_inc(w2_done, 1)

            def untranspose(g):
                pe.wait_ge(added, (g + 1) * (E - 1))
                wait_count(pe, t_read, g)
                for t in range(TPB):
                    ins = nc.tensor.transpose(ps_t[:, t, :], yT[:, t * P:(t + 1) * P], ident[:])
                ins.then_inc(t_full, 1)

            def body_b(g):
                for j in range(CH):
                    e, f = divmod(j, FC)
                    wait_count(pe, h_done, g * CH + (j - 3) if j >= 4 else g * CH)
                    dst = ps_h[:, j % 4, :]
                    cols = slice(f * P, (f + 1) * P)
                    xh, xl = x2_high[:, bass.ds(g * BT, BT)], x2_low[:, bass.ds(g * BT, BT)]
                    mm(dst, w_high[:, e, cols], xh, start=True, stop=False)
                    mm(dst, w_high[:, e, cols], xl, start=False, stop=False)
                    mm(dst, w_low[:, e, cols], xh, start=False, stop=True).then_inc(h_full, 1)
                    if f == 1:
                        wait_count(pe, wrow_done, g * E + e)
                        mm(ps_w[:], sel[:, e, :], expert_wT[:, bass.ds(g * BT, BT)], start=True, stop=True).then_inc(wrow_full, 1)
                    if j == 2 and not (isinstance(g, int) and g == 0):
                        untranspose(g - 1)
                    if j >= LAG:
                        second(g, j - LAG)
                for j in range(CH - LAG, CH):
                    second(g, j)
            loop_b(pe, body_b)
            untranspose(NB - 1)


def kernel(**inputs):
    import numpy as np
    import concourse.bacc as bacc
    from concourse.bass_utils import run_bass_kernel_spmd

    v = {k: np.ascontiguousarray(x) for k, x in inputs.items()}

    def stack(w, axis_last):
        w = w.reshape(SLABS, ROWS, HD, axis_last)
        out = np.zeros((SLABS, ROWS, COMBOS, HD, axis_last), w.dtype)
        for c in range(3):
            out[:, :, c] = w
        return out.reshape(SLABS * P, axis_last)

    bq = stack(v["L0_xattn_bq"].reshape(D, 1), 1).reshape(SLABS, ROWS, COMBOS, HD)
    bk = stack(v["L0_xattn_bk"].reshape(D, 1), 1).reshape(SLABS, ROWS, COMBOS, HD)
    bk[:, 0, 3, 0:2] = 1.0
    low = np.zeros((2, SLABS, ROWS, COMBOS, HD), np.float32)
    low[0, :, :, 1] = 1.0
    low[1, :, :, 2] = 1.0
    sel = np.zeros((P, E, P), np.uint8)
    for e in range(E):
        for j in range(3):
            sel[E * j + e, e, :] = 1
    w2 = v["L0_ffn_W2"].reshape(E, FC, P, D).transpose(0, 2, 1, 3).reshape(E, P, FC * D)
    arrays = {
        "x": v["x"].reshape(TOK, D),
        "ctx": v["ctx_1024"].reshape(TOK, D),
        "mask": v["mask_BxSxS2_bk1"].view(np.int32),
        "wqk": np.concatenate([stack(v["L0_xattn_Wq"], D).T, stack(v["L0_xattn_Wk"], D).T], 1),
        "bqk": np.concatenate([bk.reshape(SLABS, P), bq.reshape(SLABS, P)], 0).T,
        "low_rows": low.reshape(2 * SLABS, P).T,
        "wvT": v["L0_xattn_Wv"].T,
        "woT": v["L0_xattn_Wo"].T,
        "bv": v["L0_xattn_bv"].reshape(1, D),
        "bo": v["L0_xattn_bo"].reshape(1, D),
        "g": np.concatenate([v["g_xattn"], v["g_ffn"]]).reshape(1, 2),
        "w_ffn": np.concatenate([v["L0_ffn_W1"], w2, w2[0:1]], 0),
        "b1": v["L0_ffn_b1"].reshape(CH, P).T,
        "b2": v["L0_ffn_b2"].T,
        "wg": np.concatenate([v["L0_ffn_Wg"], v["L0_ffn_Wt"]], 1),
        "bg": np.concatenate([v["L0_ffn_bg"], v["L0_ffn_bt"]]).reshape(1, NGATE),
        "ident": np.eye(P, dtype=np.float32),
        "sel": sel.reshape(P, E * P).view(np.int32),
    }
    arrays["ctx"] = np.concatenate([arrays["ctx"], arrays["ctx"][0:GT]], 0)
    arrays["mask"] = np.concatenate([arrays["mask"], arrays["mask"][0:GB]], 0)
    nc = bacc.Bacc("TRN2", target_bir_lowering=False, num_devices=1)
    feed, aps = {}, {}
    for name, arr in arrays.items():
        arr = np.ascontiguousarray(arr)
        feed[f"in_{name}"] = arr
        aps[name] = nc.dram_tensor(f"in_{name}", arr.shape, mybir.dt.from_np(arr.dtype), kind="ExternalInput").ap()
    aps["out"] = nc.dram_tensor("out_y", (TOK, D), F32, kind="ExternalOutput").ap()
    gated_block(nc, aps)
    r = run_bass_kernel_spmd(nc, [feed], core_ids=[0])
    return r.results[0]["out_y"].reshape(B, S, D)
```
